# Optimizing a Trainium2 kernel written in Bass

```python
import numpy as np
import jax
import jax.numpy as jnp

def _softmax(x, axis=-1):
    return jax.nn.softmax(x, axis=axis)

def _gelu(x):
    return jax.nn.gelu(x, approximate=True)

def _silu(x):
    return jax.nn.silu(x)

def _sigmoid(x):
    return jax.nn.sigmoid(x)

def _layernorm(x, axis=-1, eps=1e-05):
    m = jnp.mean(x, axis=axis, keepdims=True)
    v = jnp.var(x, axis=axis, keepdims=True)
    return (x - m) / jnp.sqrt(v + eps)

def _scatter_add(tgt, idx, src, axis=0):
    return tgt.at[idx].add(src)

def _segment_sum(src, seg, n):
    return jax.ops.segment_sum(src, seg, n)
kernel_name = 'mk_gnn_resnorm_d4_gnn_r8_462daf'

def setup_inputs(seed: int=0):
    np.random.seed(seed)
    _w = jnp.asarray

    def _rec_inputs():
        import jax
        import jax.numpy as jnp
        _gk = jax.random.key(seed)
        x = -0.000202 + 1 * jax.random.normal(jax.random.fold_in(_gk, 1), (6250, 128), jnp.float32)
        src = jax.random.randint(jax.random.fold_in(_gk, 2), (100000,), 0, 6250, jnp.int32)
        dst = jnp.minimum((6250 * jax.random.uniform(jax.random.fold_in(_gk, 3), (100000,)) ** 2.0).astype(jnp.int32), 49999)
        _o = jnp.argsort(dst, stable=True)
        src = src[_o]
        dst = dst[_o]
        edge_attr_64 = 0.000189758 + 1.00013 * jax.random.normal(jax.random.fold_in(_gk, 12), (100000, 64), jnp.float32)
        edge_weight = jax.random.uniform(jax.random.fold_in(_gk, 14), (100000,), jnp.float32, 0.0, 1)
        return (x, src, dst, edge_attr_64, edge_weight)
    x, src, dst, edge_attr_64, edge_weight = _rec_inputs()

    def _L0_gnn_setup():
        import jax, jax.numpy as jnp
        import numpy as np
        N_NODES = 6250
        key = jax.random.key(seed)
        k1, k2, k3, k4 = jax.random.split(key, 4)
        features = jax.random.normal(k1, (N_NODES, 128), dtype=jnp.float32)
        edge_weight = jax.random.uniform(k2, (100000,), dtype=jnp.float32)
        edge_src = jax.random.randint(k3, (100000,), 0, N_NODES, dtype=jnp.int64)
        edge_dst = jax.random.randint(k4, (100000,), 0, N_NODES, dtype=jnp.int64)
        return {'features': features, 'edge_weight': edge_weight, 'edge_src': edge_src, 'edge_dst': edge_dst}
    _L0_gnn_all = _L0_gnn_setup()
    _L0_gnn_in = {k: v for k, v in _L0_gnn_all.items() if k in ()}
    del _L0_gnn_all

    def _L1_gnn_setup():
        import jax, jax.numpy as jnp
        import numpy as np
        N, E, D = (6250, 100000, 128)
        H, C = (8, 16)
        NEG_SLOPE = 0.15

        def _layernorm(x, g, b, eps=1e-05):
            mu = jnp.mean(x, axis=-1, keepdims=True)
            var = jnp.mean(jnp.square(x - mu), axis=-1, keepdims=True)
            return (x - mu) * jax.lax.rsqrt(var + eps) * g + b
        key = jax.random.key(seed)
        ks = jax.random.split(key, 8)
        x = jax.random.normal(ks[0], (N, D), dtype=jnp.float32)
        edge_index = jax.random.randint(ks[1], (2, E), 0, N, dtype=jnp.int32)
        s = 1.0 / np.sqrt(D)
        return {'x': x, 'edge_index': edge_index, 'ln_g': jnp.ones((D,), jnp.float32), 'ln_b': jnp.zeros((D,), jnp.float32), 'W_l': jax.random.normal(ks[2], (D, H * C), jnp.float32) * s, 'b_l': jnp.zeros((H * C,), jnp.float32), 'W_r': jax.random.normal(ks[3], (D, H * C), jnp.float32) * s, 'b_r': jnp.zeros((H * C,), jnp.float32), 'att': jax.random.normal(ks[4], (H, C), jnp.float32) * (1.0 / np.sqrt(C)), 'bias': jnp.zeros((H * C,), jnp.float32)}
    _L1_gnn_all = _L1_gnn_setup()
    _L1_gnn_in = {k: v for k, v in _L1_gnn_all.items() if k in ('ln_g', 'ln_b', 'W_l', 'b_l', 'W_r', 'b_r', 'att', 'bias')}
    del _L1_gnn_all

    def _L2_gnn_setup():
        import jax, jax.numpy as jnp
        import numpy as np
        N_NODES = 6250
        N_EDGES = 100000
        HIDDEN = 128
        REL = 64

        def _layer_norm(x, gamma, beta, eps=1e-05):
            mu = jnp.mean(x, axis=-1, keepdims=True)
            var = jnp.mean(jnp.square(x - mu), axis=-1, keepdims=True)
            return (x - mu) * jax.lax.rsqrt(var + eps) * gamma + beta
        key = jax.random.key(seed)
        ks = jax.random.split(key, 12)
        s = lambda fan_in: 1.0 / np.sqrt(fan_in)
        inp = {'node_states': jax.random.normal(ks[0], (N_NODES, HIDDEN), dtype=jnp.float32), 'edge_index': jax.random.randint(ks[1], (2, N_EDGES), 0, N_NODES, dtype=jnp.int64), 'edge_rel_emb': jax.random.normal(ks[2], (N_EDGES, REL), dtype=jnp.float32), 'W1': jax.random.uniform(ks[3], (2 * HIDDEN + REL, HIDDEN), jnp.float32, -s(2 * HIDDEN + REL), s(2 * HIDDEN + REL)), 'b1': jax.random.uniform(ks[4], (HIDDEN,), jnp.float32, -s(2 * HIDDEN + REL), s(2 * HIDDEN + REL)), 'W2': jax.random.uniform(ks[5], (HIDDEN, HIDDEN), jnp.float32, -s(HIDDEN), s(HIDDEN)), 'b2': jax.random.uniform(ks[6], (HIDDEN,), jnp.float32, -s(HIDDEN), s(HIDDEN)), 'Wn': jax.random.uniform(ks[7], (HIDDEN, HIDDEN), jnp.float32, -s(HIDDEN), s(HIDDEN)), 'bn': jax.random.uniform(ks[8], (HIDDEN,), jnp.float32, -s(HIDDEN), s(HIDDEN)), 'gamma': jnp.ones((HIDDEN,), jnp.float32), 'beta': jnp.zeros((HIDDEN,), jnp.float32)}
        return inp
    _L2_gnn_all = _L2_gnn_setup()
    _L2_gnn_in = {k: v for k, v in _L2_gnn_all.items() if k in ('W1', 'b1', 'W2', 'b2', 'Wn', 'bn', 'gamma', 'beta')}
    del _L2_gnn_all

    def _L3_gnn_setup():
        import jax, jax.numpy as jnp
        import numpy as np
        N = 6250
        E = 100000
        D = 128
        OUT = 128

        def _elu5(x):
            return jnp.where(x > 0, x, 5.0 * jnp.expm1(x))
        key = jax.random.key(seed)
        ks = jax.random.split(key, 12)
        s = 1.0 / np.sqrt(D)
        return {'feat': jax.random.normal(ks[0], (N, D), dtype=jnp.float32), 'src': jax.random.randint(ks[1], (E,), 0, N, dtype=jnp.int32), 'dst': jax.random.randint(ks[2], (E,), 0, N, dtype=jnp.int32), 'w_self': jax.random.normal(ks[3], (D, OUT), dtype=jnp.float32) * s, 'b_self': jnp.zeros((OUT,), dtype=jnp.float32), 'w_neigh': jax.random.normal(ks[4], (D, OUT), dtype=jnp.float32) * s, 'b_neigh': jnp.zeros((OUT,), dtype=jnp.float32), 'w_id': jax.random.normal(ks[5], (D, OUT), dtype=jnp.float32) * s, 'b_id': jnp.zeros((OUT,), dtype=jnp.float32), 'a_low': jax.random.normal(ks[6], (OUT, 1), dtype=jnp.float32) * s, 'ab_low': jnp.zeros((1,), dtype=jnp.float32), 'a_high': jax.random.normal(ks[7], (OUT, 1), dtype=jnp.float32) * s, 'ab_high': jnp.zeros((1,), dtype=jnp.float32), 'a_id': jax.random.normal(ks[8], (OUT, 1), dtype=jnp.float32) * s, 'ab_id': jnp.zeros((1,), dtype=jnp.float32)}
    _L3_gnn_all = _L3_gnn_setup()
    _L3_gnn_in = {k: v for k, v in _L3_gnn_all.items() if k in ('w_self', 'b_self', 'w_neigh', 'b_neigh', 'w_id', 'b_id', 'a_low', 'ab_low', 'a_high', 'ab_high', 'a_id', 'ab_id')}
    del _L3_gnn_all
    return {'x': x, 'src': src, 'dst': dst, 'edge_attr_64': edge_attr_64, 'edge_weight': edge_weight, 'L1_gnn_ln_g': _L1_gnn_in['ln_g'], 'L1_gnn_ln_b': _L1_gnn_in['ln_b'], 'L1_gnn_W_l': _L1_gnn_in['W_l'], 'L1_gnn_b_l': _L1_gnn_in['b_l'], 'L1_gnn_W_r': _L1_gnn_in['W_r'], 'L1_gnn_b_r': _L1_gnn_in['b_r'], 'L1_gnn_att': _L1_gnn_in['att'], 'L1_gnn_bias': _L1_gnn_in['bias'], 'L2_gnn_W1': _L2_gnn_in['W1'], 'L2_gnn_b1': _L2_gnn_in['b1'], 'L2_gnn_W2': _L2_gnn_in['W2'], 'L2_gnn_b2': _L2_gnn_in['b2'], 'L2_gnn_Wn': _L2_gnn_in['Wn'], 'L2_gnn_bn': _L2_gnn_in['bn'], 'L2_gnn_gamma': _L2_gnn_in['gamma'], 'L2_gnn_beta': _L2_gnn_in['beta'], 'L3_gnn_w_self': _L3_gnn_in['w_self'], 'L3_gnn_b_self': _L3_gnn_in['b_self'], 'L3_gnn_w_neigh': _L3_gnn_in['w_neigh'], 'L3_gnn_b_neigh': _L3_gnn_in['b_neigh'], 'L3_gnn_w_id': _L3_gnn_in['w_id'], 'L3_gnn_b_id': _L3_gnn_in['b_id'], 'L3_gnn_a_low': _L3_gnn_in['a_low'], 'L3_gnn_ab_low': _L3_gnn_in['ab_low'], 'L3_gnn_a_high': _L3_gnn_in['a_high'], 'L3_gnn_ab_high': _L3_gnn_in['ab_high'], 'L3_gnn_a_id': _L3_gnn_in['a_id'], 'L3_gnn_ab_id': _L3_gnn_in['ab_id']}

def reference(x, src, dst, edge_attr_64, edge_weight, L1_gnn_ln_g, L1_gnn_ln_b, L1_gnn_W_l, L1_gnn_b_l, L1_gnn_W_r, L1_gnn_b_r, L1_gnn_att, L1_gnn_bias, L2_gnn_W1, L2_gnn_b1, L2_gnn_W2, L2_gnn_b2, L2_gnn_Wn, L2_gnn_bn, L2_gnn_gamma, L2_gnn_beta, L3_gnn_w_self, L3_gnn_b_self, L3_gnn_w_neigh, L3_gnn_b_neigh, L3_gnn_w_id, L3_gnn_b_id, L3_gnn_a_low, L3_gnn_ab_low, L3_gnn_a_high, L3_gnn_ab_high, L3_gnn_a_id, L3_gnn_ab_id):
    import jax
    import jax.numpy as jnp

    def _L0_gnn_ref(features, edge_weight, edge_src, edge_dst):
        import jax, jax.numpy as jnp
        import numpy as np
        N_NODES = 6250
        msgs = edge_weight[:, None] * features[edge_src]
        out = jax.ops.segment_sum(msgs, edge_dst, num_segments=N_NODES)
        return out

    def _L1_gnn_ref(x, edge_index, ln_g, ln_b, W_l, b_l, W_r, b_r, att, bias):
        import jax, jax.numpy as jnp
        import numpy as np
        N, E, D = (6250, 100000, 128)
        H, C = (8, 16)
        NEG_SLOPE = 0.15

        def _layernorm(x, g, b, eps=1e-05):
            mu = jnp.mean(x, axis=-1, keepdims=True)
            var = jnp.mean(jnp.square(x - mu), axis=-1, keepdims=True)
            return (x - mu) * jax.lax.rsqrt(var + eps) * g + b
        src, dst = (edge_index[0], edge_index[1])
        h = _layernorm(x, ln_g, ln_b)
        xl = (h @ W_l + b_l).reshape(N, H, C)
        xr = (h @ W_r + b_r).reshape(N, H, C)
        e = xl[src] + xr[dst]
        e_act = jnp.where(e > 0, e, NEG_SLOPE * e)
        alpha = jnp.einsum('ehc,hc->eh', e_act, att)
        m = jax.ops.segment_max(alpha, dst, num_segments=N)
        ex = jnp.exp(alpha - m[dst])
        denom = jax.ops.segment_sum(ex, dst, num_segments=N)
        a = ex / (denom[dst] + 1e-16)
        msg = xl[src] * a[:, :, None]
        out = jax.ops.segment_sum(msg, dst, num_segments=N)
        out = out.reshape(N, H * C) + bias
        h2 = jax.nn.relu(out)
        return x + h2

    def _L2_gnn_ref(node_states, edge_index, edge_rel_emb, W1, b1, W2, b2, Wn, bn, gamma, beta):
        import jax, jax.numpy as jnp
        import numpy as np
        N_NODES = 6250
        N_EDGES = 100000
        HIDDEN = 128
        REL = 64

        def _layer_norm(x, gamma, beta, eps=1e-05):
            mu = jnp.mean(x, axis=-1, keepdims=True)
            var = jnp.mean(jnp.square(x - mu), axis=-1, keepdims=True)
            return (x - mu) * jax.lax.rsqrt(var + eps) * gamma + beta
        src, dst = (edge_index[0], edge_index[1])
        m_input = jnp.concatenate([node_states[src], node_states[dst], edge_rel_emb], axis=-1)
        h = jax.nn.relu(m_input @ W1 + b1)
        messages = jax.nn.relu(h @ W2 + b2)
        agg = jax.ops.segment_sum(messages, dst, num_segments=node_states.shape[0])
        updated = node_states + jax.nn.relu(agg @ Wn + bn)
        return _layer_norm(updated, gamma, beta)

    def _L3_gnn_ref(feat, src, dst, w_self, b_self, w_neigh, b_neigh, w_id, b_id, a_low, ab_low, a_high, ab_high, a_id, ab_id):
        import jax, jax.numpy as jnp
        import numpy as np
        N = 6250
        E = 100000
        D = 128
        OUT = 128

        def _elu5(x):
            return jnp.where(x > 0, x, 5.0 * jnp.expm1(x))
        n = feat.shape[0]
        deg = jax.ops.segment_sum(jnp.ones((src.shape[0],), feat.dtype), dst, num_segments=n)
        nsum = jax.ops.segment_sum(feat[src], dst, num_segments=n)
        h_neigh = jnp.where(deg[:, None] > 0, nsum / jnp.maximum(deg, 1.0)[:, None], 0.0)
        fs = feat @ w_self + b_self
        fn = h_neigh @ w_neigh + b_neigh
        low = jax.nn.relu(fs + fn)
        high = jax.nn.relu(fs - fn)
        identity = jax.nn.relu(feat @ w_id + b_id)

        def _att(x, a, b):
            xd = jax.lax.stop_gradient(x)
            norm = jnp.linalg.norm(xd, axis=1, keepdims=True) + 1e-16
            return jax.nn.sigmoid(_elu5(xd / norm @ a + b))
        att_low = _att(low, a_low, ab_low)
        att_high = _att(high, a_high, ab_high)
        att_mlp = _att(identity, a_id, ab_id)
        return 3.0 * (att_low * low + att_high * high + att_mlp * identity)
    edge_index = jnp.stack([src, dst])
    x = _layernorm(x + _L0_gnn_ref(x, edge_weight, src, dst), axis=-1)
    x = _layernorm(x + _L1_gnn_ref(x, edge_index, L1_gnn_ln_g, L1_gnn_ln_b, L1_gnn_W_l, L1_gnn_b_l, L1_gnn_W_r, L1_gnn_b_r, L1_gnn_att, L1_gnn_bias), axis=-1)
    x = _layernorm(x + _L2_gnn_ref(x, edge_index, edge_attr_64, L2_gnn_W1, L2_gnn_b1, L2_gnn_W2, L2_gnn_b2, L2_gnn_Wn, L2_gnn_bn, L2_gnn_gamma, L2_gnn_beta), axis=-1)
    x = _layernorm(x + _L3_gnn_ref(x, src, dst, L3_gnn_w_self, L3_gnn_b_self, L3_gnn_w_neigh, L3_gnn_b_neigh, L3_gnn_w_id, L3_gnn_b_id, L3_gnn_a_low, L3_gnn_ab_low, L3_gnn_a_high, L3_gnn_ab_high, L3_gnn_a_id, L3_gnn_ab_id), axis=-1)
    return x

_drawn_inputs = setup_inputs


def setup_inputs(seed=0):
    import zlib

    import numpy as np

    out = dict(_drawn_inputs(seed))
    spreads = {'L1_gnn_ln_g': (1.0, 0.2),
     'L1_gnn_ln_b': (0.0, 0.1),
     'L1_gnn_b_l': (0.0, 0.1),
     'L1_gnn_b_r': (0.0, 0.8),
     'L1_gnn_bias': (0.0, 0.1),
     'L2_gnn_gamma': (1.0, 0.2),
     'L2_gnn_beta': (0.0, 0.1),
     'L3_gnn_b_self': (0.0, 0.1),
     'L3_gnn_b_neigh': (0.0, 0.1),
     'L3_gnn_b_id': (0.0, 0.1)}
    factors = {'L2_gnn_b1': 2.682, 'L2_gnn_bn': 2.781}
    for name, (base, spread) in spreads.items():
        noise = np.random.default_rng([zlib.crc32(name.encode()), seed]).standard_normal(out[name].shape)
        drawn = base * np.exp(spread * noise) if base else spread * noise
        out[name] = jnp.asarray(drawn.astype(out[name].dtype))
    for name, factor in factors.items():
        out[name] = (out[name] * factor).astype(out[name].dtype)
    return out
```

```python
from contextlib import ExitStack

import concourse.bass as bass
from concourse import mybir

F32 = mybir.dt.float32
I32 = mybir.dt.int32
U32 = mybir.dt.uint32
BF16 = mybir.dt.bfloat16
ALU = mybir.AluOpType
ACT = mybir.ActivationFunctionType
AX_X = mybir.AxisListType.X

NODES, EDGES, D, REL, HEADS = 6250, 100000, 128, 64, 8
P = 128
HC = D // HEADS
TQ = 4
NIT = 14
QB = 14
NQ = NIT * QB
NT = NQ * TQ
EPAD = NT * P
CH = 7
TP = NT // CH
NB = -(-NODES // P)
NPAD = NB * P
BT = 7
NBAT = NB // BT
QE = TQ * P
RING = 7
ROWW = D + 2 * HEADS
ZROW = EPAD + NT
PROWS = EPAD + 7 * P
XROWS = NPAD + P
BIG = 1.0e38
SLOPE = 0.15
EPS = 1e-5
SLOT, WEIGHT, FIRST, HI, LO = range(5)
assert NT * P >= EDGES and NB % BT == 0 and NT % CH == 0 and QB % RING == 0 and ZROW < PROWS


def gnn_program(nc, x, src_e, dst_t, prev_t, next_t, dst_e, last_row, weight_e, rel_t,
                ln_g, ln_b, W_l, b_l, W_r, b_r, att, bias,
                W1, b1, W2, b2, Wn, bn, gamma, beta,
                w_self, b_self, w_neigh, b_neigh, w_id, b_id,
                a_low, ab_low, a_high, ab_high, a_id, ab_id, out):
    with ExitStack() as ctx:
        def sb(name, shape, dt=F32):
            return ctx.enter_context(nc.sbuf_tensor(name, shape, dt))

        def sem(name):
            return ctx.enter_context(nc.semaphore(name))

        def dram(name, shape, dt=F32):
            return nc.dram_tensor(name, shape, dt, kind="Internal").ap()

        part_d = [dram(f"partial{l}", (PROWS, ROWW if l == 1 else D)) for l in range(4)]
        xl_d, a_d, x3_d = (dram(n, (NPAD, D)) for n in ("xl", "a_src", "x3"))
        xr_d, b_d = (dram(n, (XROWS + NPAD, D)) for n in ("xr_by_rank", "b_by_rank"))
        lrank_d = dram("local_rank", (NT, P), BF16)
        pen_d = dram("scan_penalties", (NT * HEADS, 2 * P))
        rank0_d = dram("first_rank", (NT, 1), I32)

        ident = sb("ident", [P, P])
        iota_row = sb("iota_row", [P, P])
        iota_col = sb("iota_col", [P, 1])
        iota_i = sb("iota_i", [P, P], I32)
        iota_ci = sb("iota_ci", [P, 1], I32)
        tri = sb("tri", [P, P])
        trieq = sb("trieq", [P, P])
        ones = sb("ones", [P, P])
        hmask = sb("hmask", [P, HEADS])
        rec = sb("rec", [P, NT, 5])
        srct = sb("srct", [P, NT + RING * TQ], I32)
        tail_i = sb("tail_i", [TP, CH], I32)
        head_i = sb("head_i", [TP, CH], I32)
        chain_m = sb("chain_m", [TP, CH * (CH + 1) // 2, TP])
        penc = sb("penc", [HEADS, 2, NT])
        node_row = sb("node_row", [P, NB + BT], I32)
        node_xr = sb("node_xr", [P, NB], I32)
        rdeg = sb("rdeg", [P, NB])
        rank0 = sb("rank0", [1, NT], I32)
        w_lr, w_ab = sb("w_lr", [P, 2 * D]), sb("w_ab", [P, 2 * D])
        b_lr = sb("b_lr", [1, 2 * D])
        lng, lnb, attc, b1c = (sb(n, [P, 1]) for n in ("lng", "lnb", "attc", "b1c"))
        att_m = sb("att_m", [P, HEADS])
        w1c = sb("w1c", [P, D])
        w2_s, wn_s = sb("w2_s", [P, D]), sb("wn_s", [P, D])
        bn_s = sb("bn_s", [1, D])
        biasg_b, b2_b, gamma_b, beta_b = (sb(n, [P, D]) for n in ("biasg_b", "b2_b", "gamma_b", "beta_b"))
        w_x, w_n = sb("w_x", [P, 3 * D]), sb("w_n", [P, 2 * D])
        b_x, b_n = sb("b_x", [1, 3 * D]), sb("b_n", [1, D])
        a_b, ab_b = sb("a_b", [P, 3 * D]), sb("ab_b", [P, 3])

        xa = sb("xa", [P, NB, D])
        srcq = sb("srcq", [P, RING * TQ], I32)
        g = sb("g", [P, RING * TQ, D])
        work = sb("work", [P, 3 * RING * QE])
        win = work[:, 0:RING * QE].rearrange("p (r f) -> p r f", f=D)
        rel = work[:, RING * QE:2 * RING * QE].rearrange("p (s e) -> p s e", e=QE)
        lrb = work[:, 2 * RING * QE:2 * RING * QE + RING * QE // 2].bitcast(BF16).rearrange(
            "p (s e) -> p s e", e=QE)
        pen = work[0:TQ * HEADS, 2 * RING * QE + RING * QE // 2:3 * RING * QE].rearrange(
            "p (s k e) -> p s k e", k=2, e=P)
        crec = sb("crec", [P, 2, TQ, 5])
        cfirst = sb("cfirst", [P, 2, TQ])
        onehot = sb("onehot", [P, 2, TQ, P])
        onehot_t = sb("onehot_t", [P, 2, QE])
        hi1 = sb("hi1", [P, 2, TQ, NB], BF16)
        lo1 = sb("lo1", [P, 2, TQ, P], BF16)
        slope = sb("slope", [P, 2, QE])
        hid = sb("hid", [P, 2, QE])
        alpha_s = sb("alpha_s", [P, 2, TQ * HEADS])
        fwd = sb("fwd", [TQ * HEADS, P])
        seg_max = sb("seg_max", [TQ * HEADS, 2, P])
        shifted = sb("shifted", [P, 2, TQ * HEADS])
        ex = sb("ex", [P, 2, TQ * HEADS])
        msg = sb("msg", [P, 2, TQ, ROWW])
        part_s = sb("part_s", [P, 2, TQ, ROWW])
        cw = CH * ROWW
        tails = work[0:TP, 0:cw].rearrange("p (c f) -> p c f", f=ROWW)
        heads = work[0:TP, cw:2 * cw].rearrange("p (c f) -> p c f", f=ROWW)
        cmax = work[0:HEADS, 2 * cw:2 * cw + 3 * NT].rearrange("p (k t) -> p k t", k=3)
        cexp = sb("cexp", [TP, 4, CH, HEADS])
        nidx = sb("nidx", [P, BT], I32)
        xidx = sb("xidx", [P, BT], I32)
        agg = sb("agg", [P, BT, ROWW])
        y7, x7, h7 = (sb(n, [P, BT, D]) for n in ("y7", "x7", "h7"))
        ht7, nt7 = sb("ht7", [P, BT, D]), sb("nt7", [P, BT, D])
        out7 = sb("out7", [P, BT, 2 * D])
        lhi = work[:, 0:BT * 3 * D].rearrange("p (b f) -> p b f", f=3 * D)
        lhw = work[:, BT * 3 * D:2 * BT * 3 * D].rearrange("p (b f) -> p b f", f=3 * D)
        lhq = work[:, 2 * BT * 3 * D:3 * BT * 3 * D].rearrange("p (b f) -> p b f", f=3 * D)
        bst = sb("bst", [P, BT, 6])
        mv = sb("mv", [P, BT, 2])
        var, std, rstd, nwt = (sb(n, [P, BT]) for n in ("var", "std", "rstd", "nwt"))
        rden = sb("rden", [P, BT, HEADS])
        z3 = sb("z3", [P, 6, BT * 3])
        hist = sb("hist", [NB, 8, P])
        histi = sb("histi", [NB, 2, P], I32)
        htot = sb("htot", [NB, 2])

        def tview(k, dt=F32):
            v = work[0:TP, k * CH * P:(k + 1) * CH * P]
            return (v if dt == F32 else v.bitcast(dt)).rearrange("p (c e) -> p c e", e=P)

        dti, dpi, dni = tview(0, I32), tview(1, I32), tview(2, I32)
        dtf, dpf, dnf = tview(3), tview(4), tview(5)
        chg, loc, lastf = tview(6), tview(7), tview(8)
        lrank, slotf, sloti = tview(9), tview(10), tview(11, I32)
        zeros = sb("zeros", [P, ROWW])
        def nview(buf, parts=P, dt=F32):
            v = buf[0:parts].rearrange("p b f -> p (b f)")
            return v if dt == F32 else v.bitcast(dt)

        dst_ei, wcol = nview(y7, dt=I32)[:, 0:NT], nview(x7)[:, 0:NT]
        lrow_i, lrow = nview(h7, TP, I32)[:, 0:NT], nview(ht7, TP)[:, 0:NT]
        hilo_i = nview(out7, dt=I32)[:, 0:2 * NT].rearrange("p (k t) -> p k t", k=2)
        lrank_b = nview(nt7, TP, BF16)[:, 0:CH * P].rearrange("p (c e) -> p c e", e=P)
        tsm = sb("tsm", [TP, 12, CH])
        rank0_s = sb("rank0_s", [TP, CH], I32)
        tail0_i = sb("tail0_i", [TP, 2, CH], I32)
        xr0_i = sb("xr0_i", [NB, P], I32)

        bank = [ctx.enter_context(nc.psum_tensor(f"bank{i}", [P, 512], F32)) for i in range(8)]

        def part_ps(l, r, t):
            if l == 1:
                return bank[4 + t // 2][:, (t % 2) * ROWW:(t % 2 + 1) * ROWW]
            return bank[4 + 2 * r][:, t * D:(t + 1) * D]

        tables_in, src_in, x_in, weights_in = (sem(n) for n in ("tables_in", "src_in", "x_in", "weights_in"))
        consts_made, zeros_made, zeroed = sem("consts_made"), sem("zeros_made"), sem("zeroed")
        prep_pe, prep_dve, rows_ready, rows_saved, rank0_in = (
            sem(n) for n in ("prep_pe", "prep_dve", "rows_ready", "rows_saved", "rank0_in"))
        pool_step = sem("pool_step")
        gathered = [sem(f"gathered{s}") for s in range(RING)]
        src_idx_ready = sem("src_idx_ready")
        partial_done, partial_copied = sem("partial_done"), sem("partial_copied")
        partial_stored = [sem(f"partial_stored{r}") for r in range(2)]
        onehot_ready = sem("onehot_ready")
        hist_ready, hist_done, hist_pe, hist_dve = (sem(n) for n in ("hist_ready", "hist_done", "hist_pe", "hist_dve"))
        loaded = {l: [sem(f"loaded{l}_{s}") for s in range(RING)] for l in (1, 2)}
        expanded = {l: sem(f"expanded{l}") for l in (1, 2)}
        onehot_t_ready = {l: sem(f"onehot_t_ready{l}") for l in (1, 2)}
        slope_ready, leaky_ready, alpha_done, alpha_copied, alpha_t_done, scan_done, max_t_done = (
            sem(n) for n in ("slope_ready", "leaky_ready", "alpha_done", "alpha_copied", "alpha_t_done",
                             "scan_done", "max_t_done"))
        shift_ready, ex_ready, weighted = (sem(n) for n in ("shift_ready", "ex_ready", "weighted"))
        hidden_ready, hidden_used, messages_ready = (sem(n) for n in ("hidden_ready", "hidden_used", "messages_ready"))
        chain_in, chain_pe, chain_dve, chain_act, chain_out = (
            sem(n) for n in ("chain_in", "chain_pe", "chain_dve", "chain_act", "chain_out"))
        node_idx_ready, node_rows = sem("node_idx_ready"), sem("node_rows")
        var_ready, std_ready = sem("var_ready"), sem("std_ready")
        norm_ready, xt_done, xt_copied, z_done, node_out = (
            sem(n) for n in ("norm_ready", "xt_done", "xt_copied", "z_done", "node_out"))
        u_read, rel_cleared = sem("u_read"), sem("rel_cleared")
        rows_stored, rank_scattered = sem("rows_stored"), sem("rank_scattered")
        state_ready, state_stored = sem("state_ready"), sem("state_stored")
        mix_done, mix_copied, square_ready, mix_read, exp_wanted, exp_ready = (
            sem(n) for n in ("mix_done", "mix_copied", "square_ready", "mix_read", "exp_wanted", "exp_ready"))
        out_ready, out_stored = sem("out_ready"), sem("out_stored")

        def uses(n, q, ring):
            return (QB // ring) * n + q // ring

        def sweep(eng, stages):
            most = max(lead for _, lead in stages)
            for i in range(-most, 0):
                for stage, lead in stages:
                    if i + lead >= 0:
                        stage(0, i + lead)
            with eng.Fori(0, NIT - 1) as n:
                for q in range(QB):
                    for stage, lead in stages:
                        stage(n, q + lead)
            for q in range(QB):
                for stage, lead in stages:
                    if q + lead < QB:
                        stage(NIT - 1, q + lead)

        def col(v):
            return v.rearrange("(p o) -> p o", o=1)

        def row(v):
            return v.rearrange("(o f) -> o f", o=1)

        def bcast(v, parts):
            return v.partition_broadcast(parts)

        block = ctx.enter_context(nc.Block())
        N_WEIGHTS = 33

        @block.sync
        def _(sp):
            by_tile = "(c p) e -> p c e"
            for view, src in ((dti, dst_t), (dpi, prev_t), (dni, next_t)):
                sp.dma_start(view, src.rearrange(by_tile, p=TP)).then_inc(tables_in, 16)
            sp.dma_start(dst_ei, dst_e).then_inc(tables_in, 16)
            sp.dma_start(lrow_i, bcast(last_row, TP)).then_inc(tables_in, 16)
            sp.dma_start(wcol, weight_e).then_inc(tables_in, 16)
            sp.dma_start(xa[:], x.rearrange("(j k) f -> k j f", k=P)).then_inc(x_in, 16)
            loads = [
                (w_lr[:, 0:D], W_l), (w_lr[:, D:], W_r), (w_ab[:, 0:D], W1[0:D, :]), (w_ab[:, D:], W1[D:2 * D, :]),
                (b_lr[:, 0:D], row(b_l)), (b_lr[:, D:], row(b_r)), (lng[:], col(ln_g)), (lnb[:], col(ln_b)),
                (attc[:], col(att.rearrange("h c -> (h c)"))), (b1c[:], col(b1)), (w1c[0:REL, :], W1[2 * D:, :]),
                (w2_s[:], W2), (wn_s[:], Wn), (bn_s[:], row(bn)),
                (biasg_b[:], bcast(bias, P)), (b2_b[:], bcast(b2, P)), (gamma_b[:], bcast(gamma, P)), (beta_b[:], bcast(beta, P)),
                (w_x[:, 0:D], w_self), (w_x[:, D:2 * D], w_self), (w_x[:, 2 * D:], w_id),
                (w_n[:, 0:D], w_neigh), (w_n[:, D:], w_neigh),
                (b_x[:, 0:D], row(b_self)), (b_x[:, D:2 * D], row(b_self)), (b_x[:, 2 * D:], row(b_id)), (b_n[:], row(b_neigh)),
                (a_b[:, 0:D], bcast(a_low.rearrange("f o -> (f o)"), P)),
                (a_b[:, D:2 * D], bcast(a_high.rearrange("f o -> (f o)"), P)),
                (a_b[:, 2 * D:], bcast(a_id.rearrange("f o -> (f o)"), P)),
                (ab_b[:, 0:1], bcast(ab_low, P)), (ab_b[:, 1:2], bcast(ab_high, P)), (ab_b[:, 2:3], bcast(ab_id, P))]
            assert len(loads) == N_WEIGHTS
            for to, of in loads:
                sp.dma_start(to, of).then_inc(weights_in, 16)
            sp.wait_ge(rows_ready, 1)
            sp.dma_start(lrank_d.rearrange(by_tile, p=TP), lrank_b).then_inc(rows_saved, 16)
            for k, of in ((0, loc), (1, lastf)):
                for c in range(CH):
                    sp.dma_start(pen_d[c * TP * HEADS:(c + 1) * TP * HEADS, k * P:(k + 1) * P].rearrange(
                        "(p h) e -> p h e", h=HEADS), of[:, c, :].unsqueeze(1).broadcast_to([TP, HEADS, P])
                    ).then_inc(rows_saved, 16)
            with nc.allow_non_contiguous_dma(reason="784 single words, once"):
                sp.dma_start(rank0_d.rearrange("(c p) o -> p (c o)", p=TP), rank0_s[:]).then_inc(rows_saved, 16)
            sp.wait_ge(rows_saved, 16 * (2 + 2 * CH))
            sp.dma_start(rank0[:], rank0_d.rearrange("t o -> o t")).then_inc(rank0_in, 16)
            sp.wait_ge(rank0_in, 16)

            def store_node_rows(to, layer):
                with sp.Fori(0, NBAT) as b:
                    sp.wait_ge(node_out, NBAT * layer + b + 2)
                    sp.dma_start(to[bass.ds(b * (BT * P), BT * P), :].rearrange("(j k) f -> k j f", k=P),
                                 out7[:, :, 0:D]).then_inc(rows_stored, 16)

            def load_windows(l, by_rank):
                def stage(n, q):
                    i, s = n * QB + q, q % RING
                    sp.wait_ge(expanded[l], i + 1)
                    _, first = nc.values_load_multi_w_load_instructions(
                        rank0[0:1, bass.ds(i * TQ, TQ)], engines=[mybir.EngineType.SP], min_val=0, max_val=NPAD,
                        skip_runtime_bounds_check_because="a rank is below the number of nodes")
                    for t in range(TQ):
                        sp.dma_start(win[:, s * TQ + t, :], by_rank[bass.ds(first[t], P), :]).then_inc(loaded[l][s], 16)
                return stage

            store_node_rows(xl_d, 0)
            sp.wait_ge(rank_scattered, 16 * NB)
            sweep(sp, [(load_windows(1, xr_d), 0)])
            store_node_rows(a_d, 1)
            sp.wait_ge(rank_scattered, 32 * NB)
            sweep(sp, [(load_windows(2, b_d), 0)])
            with sp.Fori(0, NBAT) as b:
                sp.wait_ge(state_ready, b + 1)
                sp.dma_start(x3_d[bass.ds(b * (BT * P), BT * P), :].rearrange("(j k) f -> k j f", k=P),
                             x7[:]).then_inc(state_stored, 16)
            with sp.Fori(0, NBAT) as b:
                sp.wait_ge(out_ready, b + 1)
                sp.dma_start(out[bass.ds(b * (BT * P), BT * P), :].rearrange("(j k) f -> k j f", k=P),
                             y7[:]).then_inc(out_stored, 16)
            sp.wait_ge(out_stored, 16 + 16 * NBAT)
            sp.wait_ge(rows_stored, 16 + 32 * NBAT)
            sp.wait_ge(state_stored, 16 + 16 * NBAT)
            for r in range(2):
                sp.wait_ge(partial_stored[r], 16 + 16 * 4 * NQ // 2)

        @block.gpsimd
        def _(pool):
            pool.memset(ones[:], 1.0)
            pool.memset(ident[:], 0.0)
            pool.memset(tri[:], 1.0)
            pool.memset(trieq[:], 1.0)
            pool.memset(hmask[:], 1.0)
            pool.iota(iota_i[:], [[1, P]], base=0, channel_multiplier=0)
            pool.iota(iota_ci[:], [[0, 1]], base=0, channel_multiplier=1)
            pool.iota(tail0_i[:, 0, :], [[P * TP, CH]], base=0, channel_multiplier=P)
            pool.iota(tail0_i[:, 1, :], [[TP, CH]], base=EPAD, channel_multiplier=1)
            pool.iota(xr0_i[:], [[1, P]], base=XROWS, channel_multiplier=P)
            pool.drain()
            pool.affine_select(out=ident[:], in_=ident[:], compare_op=ALU.not_equal, fill=1.0, base=0,
                               pattern=[[1, P]], channel_multiplier=-1)
            pool.affine_select(out=tri[:], in_=tri[:], compare_op=ALU.is_gt, fill=0.0, base=0,
                               pattern=[[1, P]], channel_multiplier=-1)
            pool.affine_select(out=trieq[:], in_=trieq[:], compare_op=ALU.is_ge, fill=0.0, base=0,
                               pattern=[[1, P]], channel_multiplier=-1)
            pool.affine_select(out=hmask[:], in_=hmask[:], compare_op=ALU.is_ge, fill=0.0, base=0,
                               pattern=[[-HC, HEADS]], channel_multiplier=1)
            pool.drain()
            pool.affine_select(out=hmask[:], in_=hmask[:], compare_op=ALU.is_ge, fill=0.0, base=HC - 1,
                               pattern=[[HC, HEADS]], channel_multiplier=-1)
            pool.drain()
            pool.sem_inc(consts_made, 1)

            def gather_quads(l, table):
                with pool.Fori(0, NIT) as n:
                    for q in range(QB):
                        s = q % RING
                        pool.wait_ge(src_idx_ready, NQ * l + n * QB + q + 1)
                        pool.sem_inc(pool_step, 1)
                        for t in range(TQ):
                            pool.indirect_dma_start(
                                g[:, s * TQ + t, :], None, table,
                                bass.IndirectOffsetOnAxis(srcq[:, s * TQ + t:s * TQ + t + 1].bitcast(U32), 0),
                            ).then_inc(gathered[s], 16)

            def chain(l):
                for r in range(2):
                    pool.wait_ge(partial_stored[r], 16 + 16 * (l + 1) * NQ // 2)
                w = part_d[l].shape[1]
                if l == 0:
                    pool.wait_ge(zeroed, 16 * 6)
                for buf, idx in ((tails, tail_i), (heads, head_i)):
                    for c in range(CH):
                        pool.indirect_dma_start(buf[:, c, 0:w], None, part_d[l],
                                                bass.IndirectOffsetOnAxis(idx[:, c:c + 1].bitcast(U32), 0)
                                                ).then_inc(chain_in, 16)
                pool.wait_ge(chain_dve, (1, 5, 6, 7)[l])
                for c in range(CH):
                    pool.indirect_dma_start(part_d[l], bass.IndirectOffsetOnAxis(head_i[:, c:c + 1].bitcast(U32), 0),
                                            heads[:, c, 0:w], None).then_inc(chain_out, 16)
                pool.wait_ge(chain_out, 16 * CH * (l + 1))

            def node_rows_in(l, b):
                w = part_d[l].shape[1]
                pool.wait_ge(node_idx_ready, NBAT * l + b + 1)
                pool.sem_inc(pool_step, 1)
                for r in range(BT):
                    pool.indirect_dma_start(agg[:, r, 0:w], None, part_d[l],
                                            bass.IndirectOffsetOnAxis(nidx[:, r:r + 1].bitcast(U32), 0)
                                            ).then_inc(node_rows, 16)

            def rank_rows_out(l, to, b):
                pool.wait_ge(node_out, NBAT * l + b + 2)
                pool.sem_inc(pool_step, 1)
                for r in range(BT):
                    pool.indirect_dma_start(to, bass.IndirectOffsetOnAxis(xidx[:, r:r + 1].bitcast(U32), 0),
                                            out7[:, r, D:2 * D], None).then_inc(rank_scattered, 16)

            for l, table in enumerate((x, xl_d, a_d, x3_d)):
                if l in (1, 2):
                    pool.wait_ge(rows_stored, 16 + 16 * NBAT * l)
                if l == 3:
                    pool.wait_ge(state_stored, 16 + 16 * NBAT)
                gather_quads(l, table)
                chain(l)
                if l < 2:
                    by_rank = (xr_d, b_d)[l]
                    for b in range(2):
                        node_rows_in(l, b)
                    with pool.Fori(0, NBAT - 2) as b:
                        node_rows_in(l, b + 2)
                        rank_rows_out(l, by_rank, b)
                    for b in range(NBAT - 2, NBAT):
                        rank_rows_out(l, by_rank, b)
                else:
                    with pool.Fori(0, NBAT) as b:
                        node_rows_in(l, b)

        @block.tensor
        def _(pe):
            def mm(to, lhsT, rhs, start=True, stop=True):
                return nc.tensor.matmul(to, lhsT, rhs, start=start, stop=stop, skip_group_check=True)

            def flip(to, src, stop=True):
                k = src.shape[0]
                return nc.tensor.matmul(to, src, ident[0:k, 0:k], start=True, stop=stop, is_transpose=True,
                                        skip_group_check=True)

            pe.sem_inc(partial_done, 2)
            for l in (1, 2):
                pe.sem_inc(expanded[l], RING)
            for s in (alpha_done, max_t_done, hidden_used, hist_done):
                pe.sem_inc(s, 2)
            for s in (xt_done, z_done):
                pe.sem_inc(s, 1)

            pe.wait_ge(consts_made, 1)
            pe.wait_ge(prep_dve, 1)
            mm(bank[4][0:TP, 0:CH], tri[0:TP, 0:TP], tsm[:, 0, :])
            mm(bank[4][0:TP, CH:2 * CH], ones[0:TP, 0:TP], tsm[:, 0, :]).then_inc(prep_pe, 1)
            pe.wait_ge(prep_dve, 2)
            for c in range(CH):
                at = slice((c % 4) * TP, (c % 4 + 1) * TP)
                flip(bank[c // 4][:, at], slotf[:, c, :])
                last = flip(bank[2 + c // 4][:, at], chg[:, c, :])
            last.then_inc(prep_pe, 1)
            pe.wait_ge(prep_dve, 3)
            mm(bank[3][0:NB, 0:P], zeros[:, 0:NB], zeros[:, 0:P])

            def sum_partials(l, rhs_of, rhs_ready):
                def stage(n, q):
                    i, r = n * QB + q, q % 2
                    at = NQ * l + i
                    pe.wait_ge(onehot_ready, at + 1)
                    if rhs_ready is None:
                        pe.wait_ge(gathered[q % RING], 16 * TQ * ((NQ // RING) * l + uses(n, q, RING) + 1))
                    else:
                        pe.wait_ge(rhs_ready, i + 3)
                    pe.wait_ge(partial_copied, at + (2 if l == 1 else 1))
                    for t in range(TQ):
                        last = mm(part_ps(l, r, t), onehot[:, r, t, :], rhs_of(q, t))
                    last.then_inc(partial_done, 1)
                return stage

            def gathered_rhs(q, t):
                return g[:, (q % RING) * TQ + t, :]

            def count(n, q):
                i, r = n * QB + q, q % 2
                pe.wait_ge(hist_ready, i + 1)
                for t in range(TQ):
                    last = mm(bank[3][0:NB, 0:P], hi1[:, r, t, :], lo1[:, r, t, :], start=False, stop=False)
                last.then_inc(hist_done, 1)

            def chain_sums(l, base):
                w, per = (D + HEADS, 3) if l == 1 else (D, 4)
                for c2 in range(CH):
                    to = bank[base + c2 // per][0:TP, (c2 % per) * w:(c2 % per + 1) * w]
                    for c in range(c2 + 1):
                        last = mm(to, chain_m[:, c2 * (c2 + 1) // 2 + c, :], tails[:, c, 0:w],
                                  start=(c == 0), stop=(c == c2))
                last.then_inc(chain_pe, 1)

            def to_columns(src, w, base):
                for r in range(BT):
                    last = flip(bank[base + r // 4][:, (r % 4) * P:(r % 4 + 1) * P], src[:, r, 0:w])
                return last

            def project(layer, w_cat, bias_row, width, per, wait_rows, src):
                with pe.Fori(0, NBAT) as b:
                    done = NBAT * layer + b
                    wait_rows(b)
                    pe.wait_ge(xt_copied, done + 1)
                    to_columns(src, D, 0).then_inc(xt_done, 1)
                    pe.wait_ge(xt_copied, done + 2)
                    if layer < 2:
                        pe.wait_ge(node_out, done + 1)
                    else:
                        pe.wait_ge(u_read, b + 1)
                    for r in range(BT):
                        to = bank[2 + r // per][:, (r % per) * width:(r % per + 1) * width]
                        last = mm(to, ht7[:, r, :], w_cat, stop=bias_row is None)
                        if bias_row is not None:
                            last = mm(to, ones[0:1, :], bias_row, start=False)
                    last.then_inc(z_done, 1)

            sweep(pe, [(sum_partials(0, gathered_rhs, None), 0), (count, 0)])
            pe.wait_ge(weights_in, 16 * N_WEIGHTS)
            mm(bank[5][0:1, 0:2 * D], lnb[:], w_lr[:]).then_inc(prep_pe, 1)
            pe.wait_ge(hist_dve, 1)
            mm(bank[2][0:NB, 0:2], tri[0:NB, 0:NB], htot[:]).then_inc(hist_pe, 1)
            pe.wait_ge(hist_dve, 2)
            for k in range(3):
                last = flip(bank[2][:, P + k * NB:P + (k + 1) * NB], hist[:, 5 + k, :])
            last.then_inc(hist_pe, 1)
            pe.wait_ge(chain_in, 16 * 2 * CH)
            chain_sums(0, 0)
            project(0, w_lr[:], b_lr[:], 2 * D, 2, lambda b: pe.wait_ge(norm_ready, b + 1), h7)

            def expand_gat(n, q):
                i, r, s = n * QB + q, q % 2, q % RING
                pe.wait_ge(gathered[s], 16 * TQ * (NQ // RING + uses(n, q, RING) + 1))
                pe.wait_ge(loaded[1][s], 16 * (TQ + 2) * (uses(n, q, RING) + 1))
                pe.wait_ge(onehot_t_ready[1], i + 1)
                pe.wait_ge(leaky_ready, i + 1)
                for t in range(TQ):
                    to = bank[r][:, t * P:(t + 1) * P]
                    flip(to, g[:, s * TQ + t, :], stop=False)
                    last = mm(to, win[:, s * TQ + t, :], onehot_t[:, r, t * P:(t + 1) * P], start=False)
                last.then_inc(expanded[1], 1)

            def scores(n, q):
                i, r = n * QB + q, q % 2
                pe.wait_ge(leaky_ready, i + 3)
                pe.wait_ge(alpha_copied, i + 2)
                for t in range(TQ):
                    last = mm(bank[2][:, t * HEADS:(t + 1) * HEADS], hid[:, r, t * P:(t + 1) * P], att_m[:])
                last.then_inc(alpha_done, 1)

            def scores_t(n, q):
                i, r = n * QB + q, q % 2
                pe.wait_ge(alpha_copied, i + 3)
                pe.wait_ge(scan_done, i + 1 + RING - 2)
                flip(bank[(3, 6)[r]][0:TQ * HEADS, 0:P], alpha_s[:, r, :]).then_inc(alpha_t_done, 1)

            def maxima_t(n, q):
                i, r = n * QB + q, q % 2
                pe.wait_ge(scan_done, i + 1 + RING)
                pe.wait_ge(shift_ready, i + 2)
                mm(bank[7][:, 0:TQ * HEADS], seg_max[:, r, :],
                   ident[0:TQ * HEADS, 0:TQ * HEADS]).then_inc(max_t_done, 1)

            sweep(pe, [(scores, 3), (expand_gat, 5), (scores_t, 3), (maxima_t, 2),
                       (sum_partials(1, lambda q, t: msg[:, q % 2, t, :], weighted), 1)])
            pe.wait_ge(chain_in, 16 * 4 * CH)
            for c in range(CH):
                last = flip(bank[3 + c // 4][0:HEADS, (c % 4) * TP:(c % 4 + 1) * TP],
                            tails[:, c, D + HEADS:ROWW])
            last.then_inc(chain_pe, 1)
            pe.wait_ge(chain_dve, 2)
            for c in range(CH):
                last = flip(bank[5][0:TP, c * HEADS:(c + 1) * HEADS], cmax[:, 2, c * TP:(c + 1) * TP])
            last.then_inc(chain_pe, 1)
            pe.wait_ge(chain_dve, 4)
            chain_sums(1, 0)
            project(1, w_ab[:], None, 2 * D, 2, lambda b: pe.wait_ge(norm_ready, NBAT + b + 1), h7)

            def expand_mlp(n, q):
                i, r, s = n * QB + q, q % 2, q % RING
                pe.wait_ge(loaded[2][s], 16 * (TQ + 2) * (uses(n, q, RING) + 1))
                pe.wait_ge(onehot_t_ready[2], i + 1)
                pe.wait_ge(gathered[s], 16 * TQ * (2 * NQ // RING + uses(n, q, RING) + 1))
                pe.wait_ge(hidden_ready, i + 1)
                for t in range(TQ):
                    to = bank[r][:, t * P:(t + 1) * P]
                    flip(to, g[:, s * TQ + t, :], stop=False)
                    mm(to, w1c[:], rel[:, s, t * P:(t + 1) * P], start=False, stop=False)
                    last = mm(to, win[:, s * TQ + t, :], onehot_t[:, r, t * P:(t + 1) * P], start=False)
                last.then_inc(expanded[2], 1)

            def second_layer(n, q):
                i, r = n * QB + q, q % 2
                pe.wait_ge(hidden_ready, i + 3)
                pe.wait_ge(messages_ready, i + 1)
                for t in range(TQ):
                    last = mm(bank[2 + r][:, t * D:(t + 1) * D], hid[:, r, t * P:(t + 1) * P], w2_s[:])
                last.then_inc(hidden_used, 1)

            sweep(pe, [(second_layer, 1), (expand_mlp, 2),
                       (sum_partials(2, lambda q, t: msg[:, q % 2, t, 0:D], messages_ready), 1)])
            pe.wait_ge(chain_in, 16 * 6 * CH)
            chain_sums(2, 0)
            project(2, wn_s[:], bn_s[:], D, 4, lambda b: pe.wait_ge(node_rows, 16 * BT * (2 * NBAT + b + 1)), agg)

            sweep(pe, [(sum_partials(3, gathered_rhs, None), 0)])
            pe.wait_ge(chain_in, 16 * 8 * CH)
            chain_sums(3, 0)
            with pe.Fori(0, NBAT) as b:
                pe.wait_ge(norm_ready, 2 * NBAT + b + 1)
                pe.wait_ge(xt_copied, 3 * NBAT + b + 1)
                to_columns(x7, D, 0)
                to_columns(h7, D, 2).then_inc(xt_done, 1)
                pe.wait_ge(xt_copied, 3 * NBAT + b + 2)
                for r in range(BT):
                    pe.wait_ge(mix_copied, BT * b + r + 1)
                    to = bank[4 + r % 4]
                    mm(to[:, 0:3 * D], ht7[:, r, :], w_x[:], stop=False)
                    mm(to[:, 0:2 * D], nt7[:, r, :], w_n[:], start=False, stop=False)
                    mm(to[:, 0:3 * D], ones[0:1, :], b_x[:], start=False).then_inc(mix_done, 1)

        @block.scalar
        def _(act):
            act.sem_inc(partial_copied, 2)
            act.sem_inc(alpha_copied, 2)
            act.sem_inc(ex_ready, 2)
            act.sem_inc(hidden_ready, 2)
            act.sem_inc(mix_copied, 4)
            for s in (xt_copied, node_out):
                act.sem_inc(s, 1)
            for s in partial_stored + [rows_stored, state_stored, out_stored]:
                act.sem_inc(s, 16)
            act.dma_start(srct[:], src_e).then_inc(src_in, 16)
            act.wait_ge(src_in, 16)
            for s in range(RING):
                nc.scalar.copy(srcq[:, s * TQ:(s + 1) * TQ], srct[:, s * TQ:(s + 1) * TQ]).then_inc(src_idx_ready, 1)
            act.wait_ge(zeros_made, 1)
            for l in range(4):
                w = part_d[l].shape[1]
                act.dma_start(part_d[l][EPAD:, :].rearrange("(p r) f -> p r f", p=P),
                              zeros[:, 0:w].unsqueeze(1).broadcast_to([P, 7, w])).then_inc(zeroed, 16)
            for to in (xr_d, b_d):
                act.dma_start(to[0:XROWS, :].rearrange("(p r) f -> p r f", p=P),
                              zeros[:, 0:D].unsqueeze(1).broadcast_to([P, XROWS // P, D])).then_inc(zeroed, 16)

            def put_partials(l):
                def stage(n, q):
                    i, r = n * QB + q, q % 2
                    at, w = NQ * l + i, part_d[l].shape[1]
                    act.wait_ge(partial_done, at + 3)
                    act.wait_ge(partial_stored[r], 16 * ((NQ // 2) * l + uses(n, q, 2) + 1))
                    if l == 1:
                        for h in range(2):
                            last = nc.scalar.copy(part_s[:, r, 2 * h:2 * h + 2, :],
                                                  bank[4 + h][:, 0:2 * w].rearrange("p (t f) -> p t f", f=w))
                    else:
                        last = nc.scalar.copy(part_s[:, r, :, 0:w],
                                              bank[4 + 2 * r][:, :].rearrange("p (t f) -> p t f", f=w))
                    last.then_inc(partial_copied, 1)
                    act.wait_ge(partial_copied, at + 3)
                    act.dma_start(part_d[l][bass.ds(i * QE, QE), :].rearrange("(t s) f -> s t f", s=P),
                                  part_s[:, r, :, 0:w]).then_inc(partial_stored[r], 16)
                return stage

            def refill(used, ahead):
                def stage(n, q):
                    i, s = n * QB + q, q % RING
                    act.wait_ge(used, i + 1 + ahead)
                    nc.scalar.copy(srcq[:, s * TQ:(s + 1) * TQ],
                                   srct[:, bass.ds(i * TQ + RING * TQ, TQ)]).then_inc(src_idx_ready, 1)
                return stage

            def load_columns(l):
                def stage(n, q):
                    i, s = n * QB + q, q % RING
                    act.wait_ge(expanded[l], i + 1)
                    if l == 1:
                        act.wait_ge(scan_done, i + 1)
                    act.dma_start(lrb[:, s, :], bcast(lrank_d[bass.ds(i * TQ, TQ), :].rearrange("t e -> (t e)"), P)
                                  ).then_inc(loaded[l][s], 16)
                    if l == 1:
                        act.dma_start(pen[:, s, :, :].rearrange("p k e -> p (k e)"),
                                      pen_d[bass.ds(i * TQ * HEADS, TQ * HEADS), :]).then_inc(loaded[l][s], 16)
                    else:
                        act.dma_start(rel[0:REL, s, :], rel_t[:, bass.ds(i * QE, QE)]).then_inc(loaded[l][s], 16)
                return stage

            def root(count):
                act.wait_ge(var_ready, count + 1)
                nc.scalar.activation(std[:], var[:], ACT.Sqrt).then_inc(std_ready, 1)

            def columns_out(layer, b):
                done = NBAT * layer + b
                act.wait_ge(xt_done, done + 2)
                if layer < 3:
                    act.wait_ge(z_done, done + 1)
                nc.scalar.copy(ht7[:, 0:4, :], bank[0][:, :].rearrange("p (r n) -> p r n", n=P))
                return nc.scalar.copy(ht7[:, 4:BT, :], bank[1][:, 0:3 * P].rearrange("p (r n) -> p r n", n=P))

            def rows_out(layer, b):
                done = NBAT * layer + b
                act.wait_ge(z_done, done + 2)
                act.wait_ge(rows_stored, 16 + 16 * done)
                if not (isinstance(done, int) and done == 0):
                    act.wait_ge(rank_scattered, 16 * BT * done)
                for k in range(4):
                    c = 2 if k < 3 else 1
                    nc.scalar.copy(out7[:, 2 * k:2 * k + c, :],
                                   bank[2 + k][:, 0:c * 2 * D].rearrange("p (r f) -> p r f", f=2 * D))
                nc.scalar.copy(xidx[:], node_xr[:, bass.ds(b * BT, BT)]).then_inc(node_out, 1)

            def project_out(layer, roots):
                def batch_roots(b):
                    for k in range(roots):
                        root((0, 2 * NBAT)[layer] + roots * b + k)

                def step(b):
                    batch_roots(b + 1)
                    rows_out(layer, b)
                    columns_out(layer, b + 1).then_inc(xt_copied, 1)

                batch_roots(0)
                columns_out(layer, 0).then_inc(xt_copied, 1)
                step(0)
                with act.Fori(1, NBAT - 1) as b:
                    step(b)
                rows_out(layer, NBAT - 1)

            sweep(act, [(refill(partial_done, 2), 0), (put_partials(0), 0)])
            act.wait_ge(hist_dve, 3)
            act.wait_ge(zeroed, 16 * 6)
            project_out(0, 2)

            def slopes(n, q):
                i, r = n * QB + q, q % 2
                act.wait_ge(expanded[1], i + 1 + RING)
                act.wait_ge(leaky_ready, i + 1)
                nc.scalar.mul(slope[:, r, :], bank[r][:, :], SLOPE).then_inc(slope_ready, 1)

            def copy_scores(n, q):
                i, r = n * QB + q, q % 2
                act.wait_ge(alpha_done, i + 3)
                act.wait_ge(shift_ready, i + 1)
                nc.scalar.copy(alpha_s[:, r, :], bank[2][:, 0:TQ * HEADS]).then_inc(alpha_copied, 1)

            def exponentials(n, q):
                i, r = n * QB + q, q % 2
                act.wait_ge(shift_ready, i + 3)
                act.wait_ge(weighted, i + 1)
                nc.scalar.activation(ex[:, r, :], shifted[:, r, :], ACT.Exp).then_inc(ex_ready, 1)

            sweep(act, [(slopes, 4), (copy_scores, 3), (put_partials(1), 0), (refill(weighted, 2), 1),
                        (load_columns(1), RING + 1), (exponentials, 2)])
            act.wait_ge(chain_dve, 3)
            nc.scalar.activation(cexp[:, 0], cexp[:, 0], ACT.Exp)
            nc.scalar.activation(cexp[:, 1], cexp[:, 1], ACT.Exp)
            nc.scalar.activation(cexp[:, 2], cexp[:, 2], ACT.Exp).then_inc(chain_act, 1)
            project_out(1, 1)

            def hidden(n, q):
                i, r = n * QB + q, q % 2
                act.wait_ge(expanded[2], i + 1 + RING)
                act.wait_ge(hidden_used, i + 1)
                nc.scalar.activation(hid[:, r, :], bank[r][:, :], ACT.Relu, bias=b1c[:, 0:1]).then_inc(hidden_ready, 1)

            act.wait_ge(rel_cleared, 1)
            sweep(act, [(put_partials(2), 0), (load_columns(2), RING + 1), (hidden, 2),
                        (refill(expanded[2], RING), 2)])
            columns_out(2, 0).then_inc(xt_copied, 1)
            with act.Fori(0, NBAT - 1) as b:
                root(3 * NBAT + 2 * b)
                columns_out(2, b + 1).then_inc(xt_copied, 1)
                root(3 * NBAT + 2 * b + 1)
            for k in range(2):
                root(3 * NBAT + 2 * (NBAT - 1) + k)

            sweep(act, [(refill(partial_done, 3 * NQ + 2), 0), (put_partials(3), 0)])
            with act.Fori(0, NBAT) as b:
                columns_out(3, b)
                nc.scalar.copy(nt7[:, 0:4, :], bank[2][:, :].rearrange("p (r n) -> p r n", n=P))
                nc.scalar.copy(nt7[:, 4:BT, :], bank[3][:, 0:3 * P].rearrange("p (r n) -> p r n", n=P)).then_inc(xt_copied, 1)
                act.wait_ge(mix_read, b + 1)
                for r in range(BT):
                    act.wait_ge(mix_done, BT * b + r + 1)
                    nc.scalar.activation(lhi[:, r, :], bank[4 + r % 4][:, 0:3 * D], ACT.Relu).then_inc(mix_copied, 1)
                act.drain()
                nc.scalar.activation(lhq, lhi, ACT.Square).then_inc(square_ready, 1)
                act.wait_ge(exp_wanted, 3 * b + 1)
                nc.scalar.activation(z3[:, 2, :], z3[:, 1, :], ACT.Sqrt).then_inc(exp_ready, 1)
                act.wait_ge(exp_wanted, 3 * b + 2)
                nc.scalar.activation(z3[:, 2, :], z3[:, 1, :], ACT.Exp).then_inc(exp_ready, 1)
                act.wait_ge(exp_wanted, 3 * b + 3)
                nc.scalar.activation(z3[:, 2, :], z3[:, 1, :], ACT.Exp, scale=-1.0).then_inc(exp_ready, 1)
                root(5 * NBAT + b)

        @block.vector
        def _(dve):
            v = nc.vector
            dve.sem_inc(leaky_ready, 2)
            dve.sem_inc(scan_done, RING)
            for s in (shift_ready, weighted, messages_ready):
                dve.sem_inc(s, 2)
            for s in (u_read, mix_read):
                dve.sem_inc(s, 1)
            v.memset(zeros[:], 0.0).then_inc(zeros_made, 1)
            dve.wait_ge(consts_made, 1)
            v.tensor_copy(iota_row[:], iota_i[:])
            v.tensor_copy(iota_col[:], iota_ci[:])

            dve.wait_ge(tables_in, 16 * 6)
            v.tensor_copy(dtf, dti)
            v.tensor_copy(dpf, dpi)
            v.tensor_copy(dnf, dni)
            v.tensor_copy(lrow, lrow_i)
            v.tensor_copy(tsm[:, 8, :], tail0_i[:, 0, :])
            v.tensor_copy(tsm[:, 9, :], tail0_i[:, 1, :])
            v.tensor_scalar(hilo_i[:, 0, :], dst_ei, 7, None, ALU.arith_shift_right)
            v.tensor_scalar(hilo_i[:, 1, :], dst_ei, P - 1, None, ALU.bitwise_and)
            dve.drain()
            v.tensor_copy(rec[:, :, HI], hilo_i[:, 0, :])
            v.tensor_copy(rec[:, :, LO], hilo_i[:, 1, :])
            v.tensor_tensor(chg, dtf, dpf, ALU.not_equal)
            v.tensor_tensor(lastf, dtf, dnf, ALU.not_equal)
            dve.drain()
            v.tensor_reduce(tsm[:, 0, :], chg, AX_X, ALU.add)
            v.tensor_copy(loc, chg)
            v.tensor_copy(tsm[:, 1, :], chg[:, :, 0])
            dve.drain()
            dve.sem_inc(prep_dve, 1)
            v.memset(loc[:, :, 0], 0.0)
            v.memset(chg[:, :, 0], 1.0)
            v.tensor_scalar(tsm[:, 2, :], lastf[:, :, P - 1], -1.0, 1.0, ALU.mult, ALU.add)
            dve.drain()
            for c in range(CH):
                v.tensor_tensor_scan(lrank[:, c, :], loc[:, c, :], zeros[0:TP, 0:P], 0.0, ALU.add, ALU.max)
            dve.wait_ge(prep_pe, 1)
            v.tensor_tensor_scan(tsm[:, 3, :], bank[4][0:TP, CH:2 * CH], zeros[0:TP, 0:CH], 0.0, ALU.add, ALU.max)
            dve.drain()
            v.tensor_tensor(tsm[:, 4, :], tsm[:, 3, :], bank[4][0:TP, CH:2 * CH], ALU.subtract)
            dve.drain()
            v.tensor_tensor(tsm[:, 4, :], tsm[:, 4, :], bank[4][0:TP, 0:CH], ALU.add)
            dve.drain()
            v.scalar_tensor_tensor(out=tsm[:, 4, :], in0=tsm[:, 4, :], scalar=-1.0, in1=tsm[:, 1, :], op0=ALU.add, op1=ALU.add)
            dve.drain()
            v.tensor_copy(rank0_s[:], tsm[:, 4, :])
            v.tensor_tensor(slotf, lrank, tsm[:, 4, :].unsqueeze(2).broadcast_to([TP, CH, P]), ALU.add)
            dve.drain()
            v.tensor_copy(sloti, slotf)
            dve.drain()
            v.tensor_scalar(sloti, sloti, P - 1, None, ALU.bitwise_and)
            dve.drain()
            v.tensor_copy(slotf, sloti)
            v.tensor_copy(lrank_b, lrank)
            dve.drain()
            dve.sem_inc(prep_dve, 1)
            v.tensor_scalar(loc, loc, -BIG, None, ALU.mult)
            v.tensor_scalar(lastf, lastf, -BIG, None, ALU.mult)
            v.tensor_tensor(tsm[:, 5, :], tsm[:, 8, :], slotf[:, :, P - 1], ALU.add)
            dve.drain()
            dve.sem_inc(rows_ready, 1)
            v.tensor_copy(tail_i[:], tsm[:, 5, :])
            v.scalar_tensor_tensor(out=tsm[:, 6, :], in0=tsm[:, 5, :], scalar=float(P), in1=tsm[:, 9, :],
                                   op0=ALU.add, op1=ALU.subtract)
            dve.drain()
            v.tensor_tensor(tsm[:, 6, :], tsm[:, 6, :], tsm[:, 2, :], ALU.mult)
            dve.drain()
            v.tensor_tensor(head_i[:], tsm[:, 6, :], tsm[:, 9, :], ALU.add)
            dve.wait_ge(prep_pe, 2)
            for field, k in ((SLOT, 0), (FIRST, 2)):
                v.tensor_copy(rec[:, 0:4 * TP, field], bank[k][:, 0:4 * TP])
                v.tensor_copy(rec[:, 4 * TP:NT, field], bank[k + 1][:, 0:3 * TP])
            v.tensor_copy(rec[:, :, WEIGHT], wcol)
            dve.drain()
            dve.sem_inc(prep_dve, 1)

            def one_hots(l):
                def stage(n, q):
                    i, r = n * QB + q, q % 2
                    v.tensor_copy(crec[:, r], rec[:, bass.ds(i * TQ, TQ), :])
                    dve.drain()
                    dve.wait_ge(partial_done, NQ * l + i + 1)
                    for t in range(TQ):
                        if l == 0:
                            last = v.tensor_scalar(onehot[:, r, t, :], iota_row[:], crec[:, r, t, SLOT:SLOT + 1],
                                                   crec[:, r, t, WEIGHT:WEIGHT + 1], ALU.is_equal, ALU.mult)
                        else:
                            last = v.tensor_scalar(onehot[:, r, t, :], iota_row[:], crec[:, r, t, SLOT:SLOT + 1],
                                                   None, ALU.is_equal)
                    last.then_inc(onehot_ready, 1)
                return stage

            def hist_one_hots(n, q):
                i, r = n * QB + q, q % 2
                dve.wait_ge(hist_done, i + 1)
                for t in range(TQ):
                    v.tensor_scalar(hi1[:, r, t, :], iota_row[:, 0:NB], crec[:, r, t, HI:HI + 1], None, ALU.is_equal)
                    last = v.tensor_scalar(lo1[:, r, t, :], iota_row[:], crec[:, r, t, LO:LO + 1], None, ALU.is_equal)
                last.then_inc(hist_ready, 1)

            def transposed_one_hots(l, per_quad):
                def stage(n, q):
                    i, r, s = n * QB + q, q % 2, q % RING
                    dve.wait_ge(loaded[l][s], 16 * per_quad * (uses(n, q, RING) + 1))
                    dve.wait_ge(expanded[l], i + 1 + RING - 2)
                    v.tensor_scalar(onehot_t[:, r, :], lrb[:, s, :], iota_col[:, 0:1], None,
                                    ALU.is_equal).then_inc(onehot_t_ready[l], 1)
                return stage

            def add_chain(l, base):
                per = 4
                dve.wait_ge(chain_pe, l + 1 + (2 if l > 1 else 0))
                for k in range(2):
                    c0, c1 = k * per, min(CH, (k + 1) * per)
                    v.tensor_tensor(heads[:, c0:c1, 0:D], heads[:, c0:c1, 0:D],
                                    bank[base + k][0:TP, 0:(c1 - c0) * D].rearrange("p (c f) -> p c f", f=D), ALU.add)
                dve.drain()
                dve.sem_inc(chain_dve, 1)

            def layer_norm(to, of, count):
                for r in range(BT):
                    v.bn_stats(bst[:, r, :], of[:, r, :])
                dve.drain()
                for r in range(BT):
                    v.bn_aggr(mv[:, r, :], bst[:, r, :])
                dve.drain()
                v.tensor_scalar(var[:], mv[:, :, 1], EPS, None, ALU.add).then_inc(var_ready, 1)
                dve.wait_ge(std_ready, count + 1)
                v.reciprocal(rstd[:], std[:])
                dve.drain()
                v.tensor_tensor(nwt[:], rstd[:], rstd[:], ALU.mult)
                dve.drain()
                v.tensor_tensor(nwt[:], nwt[:], var[:], ALU.mult)
                dve.drain()
                v.tensor_scalar(nwt[:], nwt[:], -0.5, 1.5, ALU.mult, ALU.add)
                dve.drain()
                v.tensor_tensor(rstd[:], rstd[:], nwt[:], ALU.mult)
                dve.drain()
                for r in range(BT):
                    v.tensor_scalar(to[:, r, :], of[:, r, :], mv[:, r, 0:1], rstd[:, r:r + 1], ALU.subtract, ALU.mult)
                dve.drain()

            def next_indices(b):
                v.tensor_copy(nidx[:], node_row[:, bass.ds(b * BT + BT, BT)]).then_inc(node_idx_ready, 1)

            def states(b):
                return xa[:, bass.ds(b * BT, BT), :]

            def bc7(v2):
                return v2.unsqueeze(1).broadcast_to([P, BT, D])

            sweep(dve, [(one_hots(0), 0), (hist_one_hots, 0)])
            for c2 in range(CH):
                for c in range(c2 + 1):
                    v.tensor_scalar(chain_m[:, c2 * (c2 + 1) // 2 + c, :], lrow[:, c2 * TP:(c2 + 1) * TP],
                                    dtf[:, c, P - 1:P], None, ALU.is_equal)
            dve.drain()
            for c in range(CH):
                k = c * (c + 1) // 2 + c
                v.tensor_tensor(chain_m[:, k, :], chain_m[:, k, :], trieq[0:TP, 0:TP], ALU.mult)
            v.memset(penc[:], -BIG)
            dve.drain()
            v.tensor_tensor(penc[:, 0, 1:], lrow[0:HEADS, 1:], lrow[0:HEADS, 0:NT - 1], ALU.not_equal)
            v.tensor_tensor(penc[:, 1, 0:NT - 1], lrow[0:HEADS, 1:], lrow[0:HEADS, 0:NT - 1], ALU.not_equal)
            dve.drain()
            v.tensor_scalar(penc[:, 0, 1:], penc[:, 0, 1:], -BIG, None, ALU.mult)
            v.tensor_scalar(penc[:, 1, 0:NT - 1], penc[:, 1, 0:NT - 1], -BIG, None, ALU.mult)
            dve.wait_ge(hist_done, NQ + 2)
            v.tensor_copy(hist[:, 0, :], bank[3][0:NB, 0:P])
            dve.drain()
            v.tensor_scalar(hist[:, 1, :], hist[:, 0, :], 0.0, None, ALU.is_gt)
            dve.drain()
            v.tensor_reduce(htot[:, 0:1], hist[:, 0, :], AX_X, ALU.add)
            v.tensor_reduce(htot[:, 1:2], hist[:, 1, :], AX_X, ALU.add)
            v.tensor_tensor_scan(hist[:, 2, :], hist[:, 0, :], zeros[0:NB, 0:P], 0.0, ALU.add, ALU.max)
            v.tensor_tensor_scan(hist[:, 3, :], hist[:, 1, :], zeros[0:NB, 0:P], 0.0, ALU.add, ALU.max)
            v.tensor_copy(hist[:, 4, :], xr0_i[:])
            dve.drain()
            dve.sem_inc(hist_dve, 1)
            dve.wait_ge(hist_pe, 1)
            v.tensor_copy(htot[:], bank[2][0:NB, 0:2])
            dve.drain()
            v.tensor_scalar(hist[:, 2, :], hist[:, 2, :], htot[:, 0:1], -1.0, ALU.add, ALU.add)
            v.scalar_tensor_tensor(out=hist[:, 3, :], in0=hist[:, 3, :], scalar=htot[:, 1:2], in1=hist[:, 1, :],
                                   op0=ALU.add, op1=ALU.subtract)
            dve.drain()
            v.tensor_copy(histi[:, 0, :], hist[:, 2, :])
            v.tensor_copy(histi[:, 1, :], hist[:, 3, :])
            dve.drain()
            v.tensor_scalar(histi[:, 0, :], histi[:, 0, :], 7, 7, ALU.arith_shift_right, ALU.logical_shift_left)
            v.tensor_scalar(histi[:, 1, :], histi[:, 1, :], P - 1, None, ALU.bitwise_and)
            dve.drain()
            v.tensor_copy(hist[:, 5, :], histi[:, 0, :])
            v.tensor_copy(hist[:, 2, :], histi[:, 1, :])
            v.tensor_tensor(hist[:, 6, :], hist[:, 3, :], hist[:, 4, :], ALU.subtract)
            v.tensor_scalar(hist[:, 7, :], hist[:, 0, :], 1.0, None, ALU.max)
            dve.drain()
            v.scalar_tensor_tensor(out=hist[:, 5, :], in0=hist[:, 5, :], scalar=float(-ZROW), in1=hist[:, 2, :],
                                   op0=ALU.add, op1=ALU.add)
            v.tensor_tensor(hist[:, 6, :], hist[:, 6, :], hist[:, 1, :], ALU.mult)
            v.reciprocal(hist[:, 7, :], hist[:, 7, :])
            dve.drain()
            v.tensor_tensor(hist[:, 5, :], hist[:, 5, :], hist[:, 1, :], ALU.mult)
            v.tensor_tensor(hist[:, 6, :], hist[:, 6, :], hist[:, 4, :], ALU.add)
            dve.drain()
            v.tensor_scalar(hist[:, 5, :], hist[:, 5, :], float(ZROW), None, ALU.add)
            dve.drain()
            dve.sem_inc(hist_dve, 1)
            dve.wait_ge(hist_pe, 2)
            v.tensor_copy(node_row[:, 0:NB], bank[2][:, P:P + NB])
            v.tensor_copy(node_row[:, NB:NB + BT], bank[2][:, P:P + BT])
            v.tensor_copy(node_xr[:], bank[2][:, P + NB:P + 2 * NB])
            v.tensor_copy(rdeg[:], bank[2][:, P + 2 * NB:P + 3 * NB])
            dve.drain()
            dve.sem_inc(hist_dve, 1)
            v.tensor_copy(nidx[:], node_row[:, 0:BT]).then_inc(node_idx_ready, 1)
            dve.wait_ge(weights_in, 16 * N_WEIGHTS)
            dve.wait_ge(prep_pe, 3)
            v.tensor_tensor(b_lr[:], b_lr[:], bank[5][0:1, 0:2 * D], ALU.add)
            v.tensor_scalar(w_lr[:], w_lr[:], lng[:, 0:1], None, ALU.mult)
            v.tensor_scalar(att_m[:], hmask[:], attc[:, 0:1], None, ALU.mult)
            v.tensor_scalar(w_n[:, D:], w_n[:, D:], -1.0, None, ALU.mult)
            v.tensor_tensor(b_x[:, 0:D], b_x[:, 0:D], b_n[:], ALU.add)
            v.tensor_tensor(b_x[:, D:2 * D], b_x[:, D:2 * D], b_n[:], ALU.subtract)
            v.memset(w1c[REL:P, :], 0.0)
            dve.drain()
            dve.wait_ge(x_in, 16)
            add_chain(0, 0)
            with dve.Fori(0, NBAT) as b:
                dve.wait_ge(node_rows, 16 * BT * (b + 1))
                v.tensor_tensor(y7[:], agg[:, :, 0:D], states(b), ALU.add)
                dve.drain()
                next_indices(b)
                layer_norm(x7, y7, 2 * b)
                v.tensor_copy(states(b), x7[:])
                dve.wait_ge(xt_done, b + 1)
                layer_norm(h7, x7, 2 * b + 1)
                dve.sem_inc(norm_ready, 1)

            def leaky(n, q):
                i, r = n * QB + q, q % 2
                dve.wait_ge(slope_ready, i + 1)
                dve.wait_ge(alpha_done, i + 1)
                v.tensor_tensor(hid[:, r, :], bank[r][:, :], slope[:, r, :], ALU.max).then_inc(leaky_ready, 1)

            def run_maxima(n, q):
                i, r, s = n * QB + q, q % 2, q % RING
                dve.wait_ge(alpha_t_done, i + 1)
                dve.wait_ge(max_t_done, i + 1)
                v.tensor_tensor_scan(fwd[:], pen[:, s, 0, :], bank[(3, 6)[r]][0:TQ * HEADS, 0:P],
                                     -BIG, ALU.add, ALU.max)
                dve.drain()
                v.tensor_tensor_scan(seg_max[:, r, ::-1], pen[:, s, 1, ::-1], fwd[:, ::-1],
                                     -BIG, ALU.add, ALU.max).then_inc(scan_done, 1)

            def shift(n, q):
                i, r = n * QB + q, q % 2
                top = bank[7][:, 0:TQ * HEADS]
                v.tensor_copy(cfirst[:, r, :], rec[:, bass.ds(i * TQ, TQ), FIRST])
                dve.drain()
                dve.wait_ge(max_t_done, i + 3)
                dve.wait_ge(ex_ready, i + 1)
                dve.wait_ge(partial_done, NQ + i + 1)
                v.tensor_tensor(msg[:, r, :, D + HEADS:], top.rearrange("p (t h) -> p t h", h=HEADS),
                                cfirst[:, r, :].unsqueeze(2).broadcast_to([P, TQ, HEADS]), ALU.mult)
                v.tensor_tensor(shifted[:, r, :], alpha_s[:, r, :], top, ALU.subtract).then_inc(shift_ready, 1)

            def weigh(n, q):
                i, r, s = n * QB + q, q % 2, q % RING
                dve.wait_ge(ex_ready, i + 3)
                exr = ex[:, r, :].rearrange("p (t h) -> p t h", h=HEADS)
                v.tensor_copy(msg[:, r, :, D:D + HEADS], exr)
                v.tensor_tensor(msg[:, r, :, 0:D].rearrange("p t (h c) -> p t h c", c=HC),
                                g[:, s * TQ:(s + 1) * TQ, :].rearrange("p t (h c) -> p t h c", c=HC),
                                exr.unsqueeze(3).broadcast_to([P, TQ, HEADS, HC]), ALU.mult).then_inc(weighted, 1)

            sweep(dve, [(weigh, 1), (run_maxima, 2), (leaky, 4), (one_hots(1), 2), (shift, 2),
                        (transposed_one_hots(1, TQ + 2), 6)])

            tail_m, head_m = tails[:, :, D + HEADS:], heads[:, :, D + HEADS:]
            dve.wait_ge(chain_pe, 2)
            v.tensor_copy(cmax[:, 0, 0:4 * TP], bank[3][0:HEADS, 0:4 * TP])
            v.tensor_copy(cmax[:, 0, 4 * TP:NT], bank[4][0:HEADS, 0:3 * TP])
            dve.drain()
            v.tensor_tensor_scan(cmax[:, 1, :], penc[:, 0, :], cmax[:, 0, :], -BIG, ALU.add, ALU.max)
            dve.drain()
            v.tensor_tensor_scan(cmax[:, 2, ::-1], penc[:, 1, ::-1], cmax[:, 1, ::-1], -BIG, ALU.add, ALU.max)
            dve.drain()
            dve.sem_inc(chain_dve, 1)
            dve.wait_ge(chain_pe, 3)
            top = bank[5][0:TP, 0:CH * HEADS].rearrange("p (c h) -> p c h", h=HEADS)
            v.tensor_tensor(cexp[:, 0], tail_m, top, ALU.subtract)
            v.tensor_tensor(cexp[:, 3], head_m, top, ALU.max)
            dve.drain()
            v.tensor_tensor(cexp[:, 1], top, cexp[:, 3], ALU.subtract)
            v.tensor_tensor(cexp[:, 2], head_m, cexp[:, 3], ALU.subtract)
            dve.drain()
            dve.sem_inc(chain_dve, 1)
            dve.wait_ge(chain_act, 1)

            def per_head(buf, c0, c1):
                return buf[:, c0:c1, 0:D].rearrange("p c (h k) -> p c h k", k=HC)

            def over_channels(k, c0, c1):
                return cexp[:, k, c0:c1, :].unsqueeze(3).broadcast_to([TP, c1 - c0, HEADS, HC])

            for buf, k in ((tails, 0), (heads, 2)):
                v.tensor_tensor(per_head(buf, 0, CH), per_head(buf, 0, CH), over_channels(k, 0, CH), ALU.mult)
                v.tensor_tensor(buf[:, :, D:D + HEADS], buf[:, :, D:D + HEADS], cexp[:, k], ALU.mult)
            v.tensor_copy(head_m, cexp[:, 3])
            dve.drain()
            dve.sem_inc(chain_dve, 1)
            dve.wait_ge(chain_pe, 4)
            for k in range(3):
                c0, c1 = 3 * k, min(CH, 3 * k + 3)
                z = bank[k][0:TP, 0:(c1 - c0) * (D + HEADS)].rearrange("p (c f) -> p c f", f=D + HEADS)
                v.tensor_tensor(per_head(tails, c0, c1), per_head(z, 0, c1 - c0), over_channels(1, c0, c1), ALU.mult)
                v.tensor_tensor(tails[:, c0:c1, D:D + HEADS], z[:, :, D:], cexp[:, 1, c0:c1, :], ALU.mult)
            dve.drain()
            v.tensor_tensor(heads[:, :, 0:D + HEADS], heads[:, :, 0:D + HEADS], tails[:, :, 0:D + HEADS], ALU.add)
            dve.drain()
            dve.sem_inc(chain_dve, 1)
            with dve.Fori(0, NBAT) as b:
                dve.wait_ge(node_rows, 16 * BT * (NBAT + b + 1))
                v.tensor_scalar(rden[:], agg[:, :, D:D + HEADS], 1e-16, None, ALU.add)
                dve.drain()
                v.reciprocal(rden[:], rden[:])
                dve.drain()
                v.tensor_tensor(y7[:].rearrange("p b (h c) -> p b h c", c=HC),
                                agg[:, :, 0:D].rearrange("p b (h c) -> p b h c", c=HC),
                                rden[:].unsqueeze(3).broadcast_to([P, BT, HEADS, HC]), ALU.mult)
                dve.drain()
                next_indices(b)
                v.tensor_tensor(y7[:], y7[:], bc7(biasg_b[:]), ALU.add)
                dve.drain()
                v.tensor_scalar(y7[:], y7[:], 0.0, None, ALU.max)
                dve.drain()
                v.scalar_tensor_tensor(out=y7[:], in0=states(b), scalar=2.0, in1=y7[:], op0=ALU.mult, op1=ALU.add)
                dve.drain()
                dve.wait_ge(xt_done, NBAT + b + 1)
                layer_norm(h7, y7, 2 * NBAT + b)
                v.tensor_copy(states(b), h7[:])
                dve.drain()
                dve.sem_inc(norm_ready, 1)

            v.memset(rel[REL:P, :, :], 0.0).then_inc(rel_cleared, 1)

            def messages(n, q):
                i, r = n * QB + q, q % 2
                dve.wait_ge(hidden_used, i + 3)
                dve.wait_ge(partial_done, 2 * NQ + i + 1)
                to = msg[:, r, :, 0:D]
                v.tensor_tensor(to, bank[2 + r][:, :].rearrange("p (t f) -> p t f", f=D),
                                b2_b[:].unsqueeze(1).broadcast_to([P, TQ, D]), ALU.add)
                dve.drain()
                v.tensor_scalar(to, to, 0.0, None, ALU.max).then_inc(messages_ready, 1)

            sweep(dve, [(messages, 1), (transposed_one_hots(2, TQ + 2), 3), (one_hots(2), 2)])
            add_chain(2, 0)

            def updated(b):
                dve.wait_ge(z_done, 2 * NBAT + b + 2)
                for k in range(2):
                    c = (4, 3)[k]
                    last = v.scalar_tensor_tensor(
                        out=y7[:, 4 * k:4 * k + c, :], in0=bank[2 + k][:, 0:c * D].rearrange("p (r f) -> p r f", f=D),
                        scalar=0.0, in1=xa[:, bass.ds(b * BT + 4 * k, c), :], op0=ALU.max, op1=ALU.add)
                last.then_inc(u_read, 1)
                dve.drain()
                layer_norm(h7, y7, 3 * NBAT + 2 * b)

            def summed(b):
                dve.wait_ge(xt_done, 2 * NBAT + b + 2)
                next_indices(b)

            def residual(b):
                v.tensor_tensor(y7[:], h7[:], bc7(gamma_b[:]), ALU.mult)
                dve.drain()
                v.tensor_tensor(y7[:], y7[:], bc7(beta_b[:]), ALU.add)
                dve.drain()
                v.tensor_tensor(y7[:], y7[:], states(b), ALU.add)
                dve.drain()
                dve.wait_ge(state_stored, 16 + 16 * b)
                layer_norm(x7, y7, 3 * NBAT + 2 * b + 1)
                dve.sem_inc(state_ready, 1)
                v.tensor_copy(states(b), x7[:])

            summed(0)
            with dve.Fori(0, NBAT - 1) as b:
                updated(b)
                summed(b + 1)
                residual(b)
            updated(NBAT - 1)
            residual(NBAT - 1)

            sweep(dve, [(one_hots(3), 0)])
            add_chain(3, 0)
            dve.wait_ge(state_stored, 16 + 16 * NBAT)
            with dve.Fori(0, NBAT) as b:
                dve.wait_ge(node_rows, 16 * BT * (3 * NBAT + b + 1))
                dve.wait_ge(xt_done, 3 * NBAT + b + 1)
                v.tensor_tensor(h7[:], agg[:, :, 0:D],
                                rdeg[:, bass.ds(b * BT, BT)].unsqueeze(2).broadcast_to([P, BT, D]), ALU.mult)
                v.tensor_copy(x7[:], states(b))
                dve.drain()
                dve.sem_inc(norm_ready, 1)
                next_indices(b)
                dve.wait_ge(mix_copied, BT * (b + 1) + 4)
                parts = "p b (k f) -> p (b k) f"
                v.tensor_tensor(lhw, lhi, a_b[:].unsqueeze(1).broadcast_to([P, BT, 3 * D]), ALU.mult)
                dve.drain()
                v.tensor_reduce(z3[:, 0, :], lhw.rearrange(parts, k=3), AX_X, ALU.add)
                dve.wait_ge(square_ready, b + 1)
                v.tensor_reduce(z3[:, 1, :], lhq.rearrange(parts, k=3), AX_X, ALU.add)
                dve.drain()
                v.tensor_scalar(z3[:, 1, :], z3[:, 1, :], 1e-34, None, ALU.max)
                dve.drain()
                dve.sem_inc(exp_wanted, 1)
                dve.wait_ge(exp_ready, 3 * b + 1)
                v.reciprocal(z3[:, 3, :], z3[:, 2, :])
                dve.drain()
                v.tensor_tensor(z3[:, 3, :], z3[:, 3, :], z3[:, 1, :], ALU.mult)
                dve.drain()
                v.tensor_tensor(z3[:, 3, :], z3[:, 3, :], z3[:, 2, :], ALU.add)
                dve.drain()
                v.tensor_scalar(z3[:, 3, :], z3[:, 3, :], 0.5, 1e-16, ALU.mult, ALU.add)
                dve.drain()
                v.reciprocal(z3[:, 3, :], z3[:, 3, :])
                dve.drain()
                v.tensor_tensor(z3[:, 0, :], z3[:, 0, :], z3[:, 3, :], ALU.mult)
                dve.drain()
                v.tensor_tensor(z3[:, 0, :].rearrange("p (b k) -> p b k", k=3),
                                z3[:, 0, :].rearrange("p (b k) -> p b k", k=3),
                                ab_b[:].unsqueeze(1).broadcast_to([P, BT, 3]), ALU.add)
                dve.drain()
                v.tensor_scalar(z3[:, 1, :], z3[:, 0, :], 0.0, None, ALU.min)
                v.tensor_scalar(z3[:, 4, :], z3[:, 0, :], 0.0, -5.0, ALU.max, ALU.add)
                dve.drain()
                dve.sem_inc(exp_wanted, 1)
                dve.wait_ge(exp_ready, 3 * b + 2)
                v.scalar_tensor_tensor(out=z3[:, 1, :], in0=z3[:, 2, :], scalar=5.0, in1=z3[:, 4, :],
                                       op0=ALU.mult, op1=ALU.add)
                dve.drain()
                dve.sem_inc(exp_wanted, 1)
                dve.wait_ge(exp_ready, 3 * b + 3)
                v.tensor_scalar(z3[:, 3, :], z3[:, 2, :], 1.0, None, ALU.add)
                dve.drain()
                v.reciprocal(z3[:, 3, :], z3[:, 3, :])
                dve.drain()
                v.tensor_tensor(lhw.rearrange(parts, k=3), lhi.rearrange(parts, k=3),
                                z3[:, 3, :].unsqueeze(2).broadcast_to([P, BT * 3, D]), ALU.mult)
                dve.drain()
                dve.sem_inc(mix_read, 1)
                dve.wait_ge(out_stored, 16 + 16 * b)
                v.tensor_tensor(h7[:], lhw[:, :, 0:D], lhw[:, :, D:2 * D], ALU.add)
                dve.drain()
                v.tensor_tensor(h7[:], h7[:], lhw[:, :, 2 * D:], ALU.add)
                dve.drain()
                v.scalar_tensor_tensor(out=h7[:], in0=h7[:], scalar=3.0, in1=states(b), op0=ALU.mult, op1=ALU.add)
                dve.drain()
                layer_norm(y7, h7, 5 * NBAT + b)
                dve.sem_inc(out_ready, 1)


def kernel(**inputs):
    import numpy as np
    import concourse.bacc as bacc
    from concourse.bass_utils import run_bass_kernel_spmd

    def flat(name, count, fill):
        a = np.asarray(inputs[name])
        return np.concatenate([a, np.full((count - a.shape[0],) + a.shape[1:], fill, a.dtype)])

    dst = flat("dst", EPAD, NODES)
    edge = np.asarray([NODES + 1], dst.dtype)
    src = flat("src", EPAD, 0).reshape(NT, P).T
    arrays = {
        "x": flat("x", NPAD, 0),
        "src_e": np.concatenate([src, src[:, 0:RING * TQ]], axis=1),
        "dst_t": dst.reshape(NT, P),
        "prev_t": np.concatenate([edge, dst[:-1]]).reshape(NT, P),
        "next_t": np.concatenate([dst[1:], edge]).reshape(NT, P),
        "dst_e": dst.reshape(NT, P).T,
        "last_row": dst.reshape(NT, P)[:, P - 1],
        "weight_e": flat("edge_weight", EPAD, 0).reshape(NT, P).T,
        "rel_t": flat("edge_attr_64", EPAD, 0).T,
    }
    for name in ("L1_gnn_ln_g", "L1_gnn_ln_b", "L1_gnn_W_l", "L1_gnn_b_l", "L1_gnn_W_r", "L1_gnn_b_r", "L1_gnn_att",
                 "L1_gnn_bias", "L2_gnn_W1", "L2_gnn_b1", "L2_gnn_W2", "L2_gnn_b2", "L2_gnn_Wn", "L2_gnn_bn",
                 "L2_gnn_gamma", "L2_gnn_beta", "L3_gnn_w_self", "L3_gnn_b_self", "L3_gnn_w_neigh", "L3_gnn_b_neigh",
                 "L3_gnn_w_id", "L3_gnn_b_id", "L3_gnn_a_low", "L3_gnn_ab_low", "L3_gnn_a_high", "L3_gnn_ab_high",
                 "L3_gnn_a_id", "L3_gnn_ab_id"):
        arrays[name[7:]] = np.asarray(inputs[name])
    arrays = {n: np.ascontiguousarray(a) for n, a in arrays.items()}

    nc = bacc.Bacc("TRN2", target_bir_lowering=False, num_devices=1)
    args = {n: nc.dram_tensor(f"in_{n}", a.shape, mybir.dt.from_np(a.dtype), kind="ExternalInput").ap()
            for n, a in arrays.items()}
    res = nc.dram_tensor("out_x", (NPAD, D), F32, kind="ExternalOutput").ap()
    gnn_program(nc, out=res, **args)
    r = run_bass_kernel_spmd(nc, [{f"in_{n}": a for n, a in arrays.items()}], core_ids=[0])
    return r.results[0]["out_x"][:NODES]
```

```python
from contextlib import ExitStack

import concourse.bass as bass
from concourse import mybir

F32 = mybir.dt.float32
I32 = mybir.dt.int32
U32 = mybir.dt.uint32
BF16 = mybir.dt.bfloat16
ALU = mybir.AluOpType
ACT = mybir.ActivationFunctionType
AX_X = mybir.AxisListType.X

NODES, EDGES, D, REL, HEADS = 6250, 100000, 128, 64, 8
P = 128
HC = D // HEADS
TQ = 4
NIT = 14
QB = 14
NQ = NIT * QB
NT = NQ * TQ
EPAD = NT * P
CH = 7
TP = NT // CH
NB = -(-NODES // P)
NPAD = NB * P
BT = 7
NBAT = NB // BT
QE = TQ * P
UNDER_WAY = 42
RING = 7
ROWW = D + 2 * HEADS
ZROW = EPAD + NT
PROWS = EPAD + 7 * P
XROWS = NPAD + P
BIG = 1.0e38
SLOPE = 0.15
EPS = 1e-5
SLOT, WEIGHT, FIRST, HI, LO = range(5)
assert NT * P >= EDGES and NB % BT == 0 and NT % CH == 0 and QB % RING == 0 and ZROW < PROWS


def gnn_program(nc, x, src_e, dst_t, prev_t, next_t, dst_e, last_row, weight_e, rel_t,
                ln_g, ln_b, W_l, b_l, W_r, b_r, att, bias,
                W1, b1, W2, b2, Wn, bn, gamma, beta,
                w_self, b_self, w_neigh, b_neigh, w_id, b_id,
                a_low, ab_low, a_high, ab_high, a_id, ab_id, out):
    with ExitStack() as ctx:
        def sb(name, shape, dt=F32):
            return ctx.enter_context(nc.sbuf_tensor(name, shape, dt))

        def sem(name):
            return ctx.enter_context(nc.semaphore(name))

        def dram(name, shape, dt=F32):
            return nc.dram_tensor(name, shape, dt, kind="Internal").ap()

        part_d = [dram(f"partial{l}", (PROWS, ROWW if l == 1 else D)) for l in range(4)]
        xl_d, a_d, x3_d = (dram(n, (NPAD, D)) for n in ("xl", "a_src", "x3"))
        xr_d, b_d = (dram(n, (XROWS + NPAD, D)) for n in ("xr_by_rank", "b_by_rank"))
        lrank_d = dram("local_rank", (NT, P), BF16)
        pen_d = dram("scan_penalties", (NT * HEADS, 2 * P))
        rank0_d = dram("first_rank", (NT, 1), I32)

        ident = sb("ident", [P, P])
        iota_row = sb("iota_row", [P, P])
        iota_col = sb("iota_col", [P, 1])
        iota_i = sb("iota_i", [P, P], I32)
        iota_ci = sb("iota_ci", [P, 1], I32)
        tri = sb("tri", [P, P])
        trieq = sb("trieq", [P, P])
        ones = sb("ones", [P, P])
        hmask = sb("hmask", [P, HEADS])
        rec = sb("rec", [P, NT, 5])
        srct = sb("srct", [P, NT + RING * TQ], I32)
        tail_i = sb("tail_i", [TP, CH], I32)
        head_i = sb("head_i", [TP, CH], I32)
        chain_m = sb("chain_m", [TP, CH * (CH + 1) // 2, TP])
        penc = sb("penc", [HEADS, 2, NT])
        node_row = sb("node_row", [P, NB + BT], I32)
        node_xr = sb("node_xr", [P, NB], I32)
        rdeg = sb("rdeg", [P, NB])
        rank0 = sb("rank0", [1, NT], I32)
        w_lr, w_ab = sb("w_lr", [P, 2 * D]), sb("w_ab", [P, 2 * D])
        biases, bias_parts = sb("biases", [3, 5 * D]), sb("bias_parts", [P, 5 * D], BF16)
        b_lr, b_u, b_n = biases[:, 0:2 * D], biases[:, 2 * D:3 * D], biases[:, 3 * D:5 * D]
        b_lr_parts, b_u_parts, b_n_parts = (bias_parts[:, f:t] for f, t in ((0, 2 * D), (2 * D, 3 * D), (3 * D, 5 * D)))
        ones_b, lnb3 = sb("ones_b", [P, P], BF16), sb("lnb3", [P, 3])
        lng, lnb, attc, b1c = (sb(n, [P, 1]) for n in ("lng", "lnb", "attc", "b1c"))
        att_m = sb("att_m", [P, HEADS])
        w1c = sb("w1c", [P, D])
        w2_s, wn_s = sb("w2_s", [P, D]), sb("wn_s", [P, D])
        biasg_b, b2_b, gamma_b, beta_b = (sb(n, [P, D]) for n in ("biasg_b", "b2_b", "gamma_b", "beta_b"))
        w_x, w_n = sb("w_x", [P, 2 * D]), sb("w_n", [P, 2 * D])
        b_x = sb("b_x", [1, 2 * D])
        a_b, ab_b = sb("a_b", [P, 3 * D]), sb("ab_b", [P, 3])

        xa = sb("xa", [P, NB, D])
        srcq = sb("srcq", [P, RING * TQ], I32)
        g = sb("g", [P, RING * TQ, D])
        work = sb("work", [P, 3 * RING * QE])
        win = work[:, 0:RING * QE].rearrange("p (r f) -> p r f", f=D)
        rel = work[:, RING * QE:2 * RING * QE].rearrange("p (s e) -> p s e", e=QE)
        lrb = work[:, 2 * RING * QE:2 * RING * QE + RING * QE // 2].bitcast(BF16).rearrange(
            "p (s e) -> p s e", e=QE)
        pen = work[0:TQ * HEADS, 2 * RING * QE + RING * QE // 2:3 * RING * QE].rearrange(
            "p (s k e) -> p s k e", k=2, e=P)
        crec = sb("crec", [P, 2, TQ, 5])
        cfirst = sb("cfirst", [P, 2, TQ])
        onehot = sb("onehot", [P, 2, TQ, P])
        onehot_t = sb("onehot_t", [P, 2, QE])
        hi1 = sb("hi1", [P, 2, TQ, NB], BF16)
        lo1 = sb("lo1", [P, 2, TQ, P], BF16)
        slope = sb("slope", [P, 2, QE])
        hid = sb("hid", [P, 2, QE])
        alpha_s = sb("alpha_s", [P, 2, TQ * HEADS])
        fwd = sb("fwd", [TQ * HEADS, P])
        seg_max = sb("seg_max", [TQ * HEADS, 2, P])
        shifted = sb("shifted", [P, 2, TQ * HEADS])
        ex = sb("ex", [P, 2, TQ * HEADS])
        msg = sb("msg", [P, 2, TQ, ROWW])
        part_s = sb("part_s", [P, 2, TQ, ROWW])
        cmax = work[0:HEADS, 0:3 * NT].rearrange("p (k t) -> p k t", k=3)
        cexp = sb("cexp", [TP, 4, CH, HEADS])
        nidx = sb("nidx", [P, BT], I32)
        xidx = sb("xidx", [P, BT], I32)
        agg = sb("agg", [P, BT, ROWW])
        y7, x7, h7 = (sb(n, [P, BT, D]) for n in ("y7", "x7", "h7"))
        ht7, nt7 = sb("ht7", [P, BT, D]), sb("nt7", [P, BT, D])
        out7 = sb("out7", [P, BT, 2 * D])
        tails = agg[0:TP]
        heads = out7[0:TP].rearrange("p b f -> p (b f)")[:, 0:CH * ROWW].rearrange("p (c f) -> p c f", f=ROWW)
        own = work[:, 0:NB * D].rearrange("p (j f) -> p j f", f=D)
        mix = work[:, NB * D:NB * D + BT * 2 * D].rearrange("p (b f) -> p b f", f=2 * D)
        mix_a = work[:, NB * D + BT * 2 * D:NB * D + 2 * BT * 2 * D].rearrange("p (b f) -> p b f", f=2 * D)
        mix_sq = out7
        bst = sb("bst", [P, BT, 6])
        mv = sb("mv", [P, 2, BT, 2])
        var, std, rstd, nshift = (sb(n, [P, 2, BT]) for n in ("var", "std", "rstd", "nshift"))
        nwt = sb("nwt", [P, BT])
        rden = sb("rden", [P, BT, HEADS])
        z_id, z_mix = sb("z_id", [P, 5, BT]), sb("z_mix", [P, 5, BT * 2])
        hist = sb("hist", [NB, 8, P])
        histi = sb("histi", [NB, 2, P], I32)
        htot = sb("htot", [NB, 2])

        def tview(k, dt=F32):
            v = work[0:TP, k * CH * P:(k + 1) * CH * P]
            return (v if dt == F32 else v.bitcast(dt)).rearrange("p (c e) -> p c e", e=P)

        dti, dpi, dni = tview(0, I32), tview(1, I32), tview(2, I32)
        dtf, dpf, dnf = tview(3), tview(4), tview(5)
        chg, loc, lastf = tview(6), tview(7), tview(8)
        lrank, slotf, sloti = tview(9), tview(10), tview(11, I32)
        zeros = sb("zeros", [P, ROWW])
        def nview(buf, parts=P, dt=F32):
            v = buf[0:parts].rearrange("p b f -> p (b f)")
            return v if dt == F32 else v.bitcast(dt)

        dst_ei, wcol = nview(y7, dt=I32)[:, 0:NT], nview(x7)[:, 0:NT]
        lrow_i, lrow = nview(h7, TP, I32)[:, 0:NT], nview(ht7, TP)[:, 0:NT]
        hilo_i = nview(out7, dt=I32)[:, 0:2 * NT].rearrange("p (k t) -> p k t", k=2)
        lrank_b = nview(nt7, TP, BF16)[:, 0:CH * P].rearrange("p (c e) -> p c e", e=P)
        tsm = sb("tsm", [TP, 12, CH])
        rank0_s = sb("rank0_s", [TP, CH], I32)
        tail0_i = sb("tail0_i", [TP, 2, CH], I32)
        xr0_i = sb("xr0_i", [NB, P], I32)

        bank = [ctx.enter_context(nc.psum_tensor(f"bank{i}", [P, 512], F32)) for i in range(8)]

        def part_ps(l, r, t):
            if l == 1:
                return bank[4 + t // 2][:, (t % 2) * ROWW:(t % 2 + 1) * ROWW]
            return bank[4 + 2 * r][:, t * D:(t + 1) * D]

        tables_in, src_in, x_in, weights_in = (sem(n) for n in ("tables_in", "src_in", "x_in", "weights_in"))
        consts_made, zeros_made, zeroed = sem("consts_made"), sem("zeros_made"), sem("zeroed")
        prep_pe, prep_dve, rows_ready, rows_saved, rank0_in = (
            sem(n) for n in ("prep_pe", "prep_dve", "rows_ready", "rows_saved", "rank0_in"))
        pool_step = sem("pool_step")
        gathered = [sem(f"gathered{s}") for s in range(RING)]
        src_idx_ready = sem("src_idx_ready")
        partial_done, partial_copied = sem("partial_done"), sem("partial_copied")
        partial_stored = [sem(f"partial_stored{r}") for r in range(2)]
        onehot_ready = sem("onehot_ready")
        hist_ready, hist_done, hist_pe, hist_dve = (sem(n) for n in ("hist_ready", "hist_done", "hist_pe", "hist_dve"))
        loaded = {l: [sem(f"loaded{l}_{s}") for s in range(RING)] for l in (1, 2)}
        expanded = {l: sem(f"expanded{l}") for l in (1, 2)}
        onehot_t_ready = {l: sem(f"onehot_t_ready{l}") for l in (1, 2)}
        slope_ready, leaky_ready, alpha_done, alpha_copied, alpha_t_done, scan_done, max_t_done = (
            sem(n) for n in ("slope_ready", "leaky_ready", "alpha_done", "alpha_copied", "alpha_t_done",
                             "scan_done", "max_t_done"))
        shift_ready, ex_ready, weighted = (sem(n) for n in ("shift_ready", "ex_ready", "weighted"))
        hidden_ready, hidden_used, messages_ready = (sem(n) for n in ("hidden_ready", "hidden_used", "messages_ready"))
        tails_in, last_tails_in, heads_in, chain_pe, chain_dve, chain_act, chain_out = (
            sem(n) for n in ("tails_in", "last_tails_in", "heads_in", "chain_pe", "chain_dve", "chain_act", "chain_out"))
        node_idx_ready, node_rows = sem("node_idx_ready"), sem("node_rows")
        var_ready, std_ready = sem("var_ready"), sem("std_ready")
        norm_ready, xt_done, xt_copied, z_done, node_out = (
            sem(n) for n in ("norm_ready", "xt_done", "xt_copied", "z_done", "node_out"))
        update_read, rel_cleared = sem("update_read"), sem("rel_cleared")
        rows_stored, rank_scattered = sem("rows_stored"), sem("rank_scattered")
        state_ready, state_stored = sem("state_ready"), sem("state_stored")
        scale_ready, centred, applied, split_ready = (sem(n) for n in ("scale_ready", "centred", "applied", "split_ready"))
        mix_done, mix_copied, square_ready, mix_read, exp_wanted, exp_ready = (
            sem(n) for n in ("mix_done", "mix_copied", "square_ready", "mix_read", "exp_wanted", "exp_ready"))
        out_ready, out_stored = sem("out_ready"), sem("out_stored")

        def uses(n, q, ring):
            return (QB // ring) * n + q // ring

        def sweep(eng, stages, span=1, beside=None):
            most = max(lead for _, lead in stages)
            for i in range(-most, 0):
                for stage, lead in stages:
                    if i + lead >= 0:
                        stage(0, i + lead)
            turns = NIT // span
            with eng.Fori(0, turns - 1) as m:
                for q in range(span * QB):
                    for stage, lead in stages:
                        stage(m * span, q + lead)
                    if beside is not None:
                        beside(m, q)
            for q in range(span * QB):
                for stage, lead in stages:
                    if q + lead < span * QB:
                        stage(NIT - span, q + lead)
                if beside is not None:
                    beside(turns - 1, q)

        (STEP_STATES, STEP_FLIP, STEP_COLUMNS, STEP_PROJECT, STEP_SPLIT, STEP_DOTS, STEP_ROOT, STEP_SCORE,
         STEP_EXP, STEP_ELU, STEP_EXP2, STEP_MIX) = range(1, 25, 2)
        assert NIT // 2 == NBAT

        def is_batch(b, batch):
            return isinstance(b, int) and b == batch

        def states(b):
            return xa[:, bass.ds(b * BT, BT), :]

        def col(v):
            return v.rearrange("(p o) -> p o", o=1)

        def row(v):
            return v.rearrange("(o f) -> o f", o=1)

        def bcast(v, parts):
            return v.partition_broadcast(parts)

        block = ctx.enter_context(nc.Block())
        N_WEIGHTS = 31

        @block.sync
        def _(sp):
            by_tile = "(c p) e -> p c e"
            for view, src in ((dti, dst_t), (dpi, prev_t), (dni, next_t)):
                sp.dma_start(view, src.rearrange(by_tile, p=TP)).then_inc(tables_in, 16)
            sp.dma_start(dst_ei, dst_e).then_inc(tables_in, 16)
            sp.dma_start(lrow_i, bcast(last_row, TP)).then_inc(tables_in, 16)
            sp.dma_start(wcol, weight_e).then_inc(tables_in, 16)
            sp.dma_start(xa[:], x.rearrange("(j k) f -> k j f", k=P)).then_inc(x_in, 16)
            loads = [
                (w_lr[:, 0:D], W_l), (w_lr[:, D:], W_r), (w_ab[:, 0:D], W1[0:D, :]), (w_ab[:, D:], W1[D:2 * D, :]),
                (b_lr[:, 0:D], bcast(b_l, 3)), (b_lr[:, D:], bcast(b_r, 3)), (lng[:], col(ln_g)), (lnb[:], col(ln_b)),
                (attc[:], col(att.rearrange("h c -> (h c)"))), (b1c[:], col(b1)), (w1c[0:REL, :], W1[2 * D:, :]),
                (w2_s[:], W2), (wn_s[:], Wn), (b_u, bcast(bn, 3)),
                (biasg_b[:], bcast(bias, P)), (b2_b[:], bcast(b2, P)), (gamma_b[:], bcast(gamma, P)), (beta_b[:], bcast(beta, P)),
                (w_x[:, 0:D], w_self), (w_x[:, D:], w_id),
                (w_n[:, 0:D], w_neigh), (w_n[:, D:], w_neigh),
                (b_x[:, 0:D], row(b_self)), (b_x[:, D:], row(b_id)), (b_n[:, 0:D], bcast(b_neigh, 3)),
                (a_b[:, 0:D], bcast(a_low.rearrange("f o -> (f o)"), P)),
                (a_b[:, D:2 * D], bcast(a_high.rearrange("f o -> (f o)"), P)),
                (a_b[:, 2 * D:], bcast(a_id.rearrange("f o -> (f o)"), P)),
                (ab_b[:, 0:1], bcast(ab_low, P)), (ab_b[:, 1:2], bcast(ab_high, P)), (ab_b[:, 2:3], bcast(ab_id, P))]
            assert len(loads) == N_WEIGHTS
            for to, of in loads:
                sp.dma_start(to, of).then_inc(weights_in, 16)
            sp.wait_ge(rows_ready, 1)
            sp.dma_start(lrank_d.rearrange(by_tile, p=TP), lrank_b).then_inc(rows_saved, 16)
            with nc.allow_non_contiguous_dma(reason="784 single words, once"):
                sp.dma_start(rank0_d.rearrange("(c p) o -> p (c o)", p=TP), rank0_s[:]).then_inc(rows_saved, 16)
            sp.wait_ge(rows_saved, 16 * 2)
            sp.dma_start(rank0[:], rank0_d.rearrange("t o -> o t")).then_inc(rank0_in, 16)
            sp.wait_ge(rank0_in, 16)
            sp.wait_ge(partial_done, 2 + UNDER_WAY)
            for k, of in ((0, loc), (1, lastf)):
                for c in range(CH):
                    sp.dma_start(pen_d[c * TP * HEADS:(c + 1) * TP * HEADS, k * P:(k + 1) * P].rearrange(
                        "(p h) e -> p h e", h=HEADS), of[:, c, :].unsqueeze(1).broadcast_to([TP, HEADS, P])
                    ).then_inc(rows_saved, 16)
            sp.wait_ge(zeros_made, 1)
            for l in range(4):
                w = part_d[l].shape[1]
                sp.dma_start(part_d[l][EPAD:, :].rearrange("(p r) f -> p r f", p=P),
                             zeros[:, 0:w].unsqueeze(1).broadcast_to([P, 7, w])).then_inc(zeroed, 16)
            for to in (xr_d, b_d):
                sp.dma_start(to[0:XROWS, :].rearrange("(p r) f -> p r f", p=P),
                             zeros[:, 0:D].unsqueeze(1).broadcast_to([P, XROWS // P, D])).then_inc(zeroed, 16)
            sp.wait_ge(rows_saved, 16 * (2 + 2 * CH))

            def store_node_rows(to, layer):
                with sp.Fori(0, NBAT) as b:
                    sp.wait_ge(node_out, NBAT * layer + b + 2)
                    sp.dma_start(to[bass.ds(b * (BT * P), BT * P), :].rearrange("(j k) f -> k j f", k=P),
                                 out7[:, :, 0:D]).then_inc(rows_stored, 16)

            def load_windows(l, by_rank):
                def stage(n, q):
                    i, s = n * QB + q, q % RING
                    sp.wait_ge(expanded[l], i + 1)
                    _, first = nc.values_load_multi_w_load_instructions(
                        rank0[0:1, bass.ds(i * TQ, TQ)], engines=[mybir.EngineType.SP], min_val=0, max_val=NPAD,
                        skip_runtime_bounds_check_because="a rank is below the number of nodes")
                    for t in range(TQ):
                        sp.dma_start(win[:, s * TQ + t, :], by_rank[bass.ds(first[t], P), :]).then_inc(loaded[l][s], 16)
                return stage

            store_node_rows(xl_d, 0)
            sp.wait_ge(rank_scattered, 16 * NB)
            sweep(sp, [(load_windows(1, xr_d), 0)])
            store_node_rows(a_d, 1)
            sp.wait_ge(rank_scattered, 32 * NB)
            sweep(sp, [(load_windows(2, b_d), 0)])
            with sp.Fori(0, NBAT) as b:
                sp.wait_ge(state_ready, b + 1)
                sp.dma_start(x3_d[bass.ds(b * (BT * P), BT * P), :].rearrange("(j k) f -> k j f", k=P),
                             x7[:]).then_inc(state_stored, 16)
            with sp.Fori(0, NBAT) as b:
                sp.wait_ge(out_ready, b + 1)
                sp.dma_start(out[bass.ds(b * (BT * P), BT * P), :].rearrange("(j k) f -> k j f", k=P),
                             x7[:]).then_inc(out_stored, 16)
            sp.wait_ge(out_stored, 16 + 16 * NBAT)
            sp.wait_ge(rows_stored, 16 + 32 * NBAT)
            sp.wait_ge(state_stored, 16 + 16 * NBAT)
            for r in range(2):
                sp.wait_ge(partial_stored[r], 16 + 16 * 4 * NQ // 2)

        @block.gpsimd
        def _(pool):
            pool.memset(ones[:], 1.0)
            pool.memset(ones_b[:], 1.0)
            pool.memset(bias_parts[:], 0.0)
            pool.memset(ident[:], 0.0)
            pool.memset(tri[:], 1.0)
            pool.memset(trieq[:], 1.0)
            pool.memset(hmask[:], 1.0)
            pool.iota(iota_i[:], [[1, P]], base=0, channel_multiplier=0)
            pool.iota(iota_ci[:], [[0, 1]], base=0, channel_multiplier=1)
            pool.iota(tail0_i[:, 0, :], [[P * TP, CH]], base=0, channel_multiplier=P)
            pool.iota(tail0_i[:, 1, :], [[TP, CH]], base=EPAD, channel_multiplier=1)
            pool.iota(xr0_i[:], [[1, P]], base=XROWS, channel_multiplier=P)
            pool.drain()
            pool.affine_select(out=ident[:], in_=ident[:], compare_op=ALU.not_equal, fill=1.0, base=0,
                               pattern=[[1, P]], channel_multiplier=-1)
            pool.affine_select(out=tri[:], in_=tri[:], compare_op=ALU.is_gt, fill=0.0, base=0,
                               pattern=[[1, P]], channel_multiplier=-1)
            pool.affine_select(out=trieq[:], in_=trieq[:], compare_op=ALU.is_ge, fill=0.0, base=0,
                               pattern=[[1, P]], channel_multiplier=-1)
            pool.affine_select(out=hmask[:], in_=hmask[:], compare_op=ALU.is_ge, fill=0.0, base=0,
                               pattern=[[-HC, HEADS]], channel_multiplier=1)
            pool.drain()
            pool.affine_select(out=hmask[:], in_=hmask[:], compare_op=ALU.is_ge, fill=0.0, base=HC - 1,
                               pattern=[[HC, HEADS]], channel_multiplier=-1)
            pool.drain()
            pool.sem_inc(consts_made, 1)

            def gather_quads(l, table):
                with pool.Fori(0, NIT) as n:
                    for q in range(QB):
                        s = q % RING
                        pool.wait_ge(src_idx_ready, NQ * l + n * QB + q + 1)
                        pool.sem_inc(pool_step, 1)
                        for t in range(TQ):
                            pool.indirect_dma_start(
                                g[:, s * TQ + t, :], None, table,
                                bass.IndirectOffsetOnAxis(srcq[:, s * TQ + t:s * TQ + t + 1].bitcast(U32), 0),
                            ).then_inc(gathered[s], 16)

            def chain(l):
                w = part_d[l].shape[1]

                early = (CH - 1) * TP

                def rows_in(buf, idx, c, of, done):
                    pool.indirect_dma_start(buf[:, c, 0:w], None, of,
                                            bass.IndirectOffsetOnAxis(idx[:, c:c + 1].bitcast(U32), 0)).then_inc(done, 16)

                for r in range(2):
                    pool.wait_ge(partial_stored[r], 16 + 16 * ((NQ // 2) * l + early // TQ // 2))
                for c in range(CH - 1):
                    rows_in(tails, tail_i, c, part_d[l][0:early * P, :], tails_in)
                for r in range(2):
                    pool.wait_ge(partial_stored[r], 16 + 16 * (l + 1) * NQ // 2)
                if l == 0:
                    pool.wait_ge(zeroed, 16 * 6)
                rows_in(tails, tail_i, CH - 1, part_d[l], last_tails_in)
                if l == 1:
                    for c in range(CH):
                        rows_in(heads, head_i, c, part_d[l], heads_in)
                    pool.wait_ge(chain_dve, 6)
                for c in range(CH):
                    if l != 1 and c in (0, 4):
                        pool.wait_ge(chain_dve, {0: 1, 2: 7, 3: 9}[l] + c // 4)
                    pool.indirect_dma_start(part_d[l], bass.IndirectOffsetOnAxis(head_i[:, c:c + 1].bitcast(U32), 0),
                                            heads[:, c, 0:w], None, **({} if l == 1 else {"compute_op": ALU.add})
                                            ).then_inc(chain_out, 16)
                pool.wait_ge(chain_out, 16 * CH * (l + 1))

            def node_rows_in(l, b):
                w = part_d[l].shape[1]
                pool.wait_ge(node_idx_ready, NBAT * l + b + 1)
                pool.sem_inc(pool_step, 1)
                for r in range(BT):
                    pool.indirect_dma_start(agg[:, r, 0:w], None, part_d[l],
                                            bass.IndirectOffsetOnAxis(nidx[:, r:r + 1].bitcast(U32), 0)
                                            ).then_inc(node_rows, 16)

            def rank_rows_out(l, to, b):
                pool.wait_ge(node_out, NBAT * l + b + 2)
                pool.sem_inc(pool_step, 1)
                for r in range(BT):
                    pool.indirect_dma_start(to, bass.IndirectOffsetOnAxis(xidx[:, r:r + 1].bitcast(U32), 0),
                                            out7[:, r, D:2 * D], None).then_inc(rank_scattered, 16)

            for l, table in enumerate((x, xl_d, a_d, x3_d)):
                if l in (1, 2):
                    pool.wait_ge(rows_stored, 16 + 16 * NBAT * l)
                if l == 3:
                    pool.wait_ge(state_stored, 16 + 16 * NBAT)
                gather_quads(l, table)
                chain(l)
                if l < 2:
                    by_rank = (xr_d, b_d)[l]
                    for b in range(2):
                        node_rows_in(l, b)
                    with pool.Fori(0, NBAT - 2) as b:
                        node_rows_in(l, b + 2)
                        rank_rows_out(l, by_rank, b)
                    for b in range(NBAT - 2, NBAT):
                        rank_rows_out(l, by_rank, b)
                else:
                    with pool.Fori(0, NBAT) as b:
                        node_rows_in(l, b)

        OWN_BANKS = (2, 3, 5, 7)

        @block.tensor
        def _(pe):
            def mm(to, lhsT, rhs, start=True, stop=True):
                return nc.tensor.matmul(to, lhsT, rhs, start=start, stop=stop, skip_group_check=True)

            def flip(to, src, stop=True):
                k = src.shape[0]
                return nc.tensor.matmul(to, src, ident[0:k, 0:k], start=True, stop=stop, is_transpose=True,
                                        skip_group_check=True)

            pe.sem_inc(partial_done, 2)
            for l in (1, 2):
                pe.sem_inc(expanded[l], RING)
            for s in (alpha_done, max_t_done, hidden_used, hist_done):
                pe.sem_inc(s, 2)
            for s in (xt_done, z_done):
                pe.sem_inc(s, 1)

            pe.wait_ge(consts_made, 1)
            pe.wait_ge(prep_dve, 1)
            mm(bank[4][0:TP, 0:CH], tri[0:TP, 0:TP], tsm[:, 0, :])
            mm(bank[4][0:TP, CH:2 * CH], ones[0:TP, 0:TP], tsm[:, 0, :]).then_inc(prep_pe, 1)
            pe.wait_ge(prep_dve, 2)
            for c in range(CH):
                at = slice((c % 4) * TP, (c % 4 + 1) * TP)
                flip(bank[c // 4][:, at], slotf[:, c, :])
                last = flip(bank[2 + c // 4][:, at], chg[:, c, :])
            last.then_inc(prep_pe, 1)
            pe.wait_ge(prep_dve, 3)
            mm(bank[3][0:NB, 0:P], zeros[:, 0:NB], zeros[:, 0:P])

            def sum_partials(l, rhs_of, rhs_ready):
                def stage(n, q):
                    i, r = n * QB + q, q % 2
                    at = NQ * l + i
                    pe.wait_ge(onehot_ready, at + 1)
                    if rhs_ready is None:
                        pe.wait_ge(gathered[q % RING], 16 * TQ * ((NQ // RING) * l + uses(n, q, RING) + 1))
                    else:
                        pe.wait_ge(rhs_ready, i + 3)
                    pe.wait_ge(partial_copied, at + (2 if l == 1 else 1))
                    for t in range(TQ):
                        last = mm(part_ps(l, r, t), onehot[:, r, t, :], rhs_of(q, t))
                    last.then_inc(partial_done, 1)
                return stage

            def gathered_rhs(q, t):
                return g[:, (q % RING) * TQ + t, :]

            def count(n, q):
                i, r = n * QB + q, q % 2
                pe.wait_ge(hist_ready, i + 1)
                for t in range(TQ):
                    last = mm(bank[3][0:NB, 0:P], hi1[:, r, t, :], lo1[:, r, t, :], start=False, stop=False)
                last.then_inc(hist_done, 1)

            def tails_ready(l, c):
                if c == 0:
                    pe.wait_ge(tails_in, 16 * (CH - 1) * (l + 1))
                if c == CH - 1:
                    pe.wait_ge(last_tails_in, 16 * (l + 1))

            def chain_sums(l):
                w, per = (D + HEADS, 3) if l == 1 else (D, 4)
                for c2 in range(CH):
                    if l != 1:
                        tails_ready(l, c2)
                    to = bank[c2 // per][0:TP, (c2 % per) * w:(c2 % per + 1) * w]
                    for c in range(c2 + 1):
                        last = mm(to, chain_m[:, c2 * (c2 + 1) // 2 + c, :], tails[:, c, 0:w],
                                  start=(c == 0), stop=(c == c2))
                    if c2 == CH - 1 or (l != 1 and c2 == per - 1):
                        last.then_inc(chain_pe, 1)

            def to_columns(src, w, base):
                for r in range(BT):
                    last = flip(bank[base + r // 4][:, (r % 4) * P:(r % 4 + 1) * P], src[:, r, 0:w])
                return last

            def project(layer, w_cat, bias_row, width, per, wait_rows, src):
                with pe.Fori(0, NBAT) as b:
                    done = NBAT * layer + b
                    wait_rows(b)
                    pe.wait_ge(xt_copied, done + 1)
                    to_columns(src, D, 0).then_inc(xt_done, 1)
                    pe.wait_ge(xt_copied, done + 2)
                    if layer < 2:
                        pe.wait_ge(node_out, done + 1)
                    else:
                        pe.wait_ge(update_read, b + 1)
                    for r in range(BT):
                        to = bank[2 + r // per][:, (r % per) * width:(r % per + 1) * width]
                        last = mm(to, ht7[:, r, :], w_cat, stop=bias_row is None)
                        if bias_row is not None:
                            last = mm(to, ones_b[:], bias_row, start=False)
                    last.then_inc(z_done, 1)

            sweep(pe, [(sum_partials(0, gathered_rhs, None), 0), (count, 0)])
            pe.wait_ge(weights_in, 16 * N_WEIGHTS)
            pe.wait_ge(prep_dve, 4)
            mm(bank[5][0:3, 0:2 * D], lnb3[:], w_lr[:]).then_inc(prep_pe, 1)
            pe.wait_ge(hist_dve, 1)
            mm(bank[2][0:NB, 0:2], tri[0:NB, 0:NB], htot[:]).then_inc(hist_pe, 1)
            pe.wait_ge(hist_dve, 2)
            for k in range(3):
                last = flip(bank[2][:, P + k * NB:P + (k + 1) * NB], hist[:, 5 + k, :])
            last.then_inc(hist_pe, 1)
            chain_sums(0)
            project(0, w_lr[:], b_lr_parts, 2 * D, 2, lambda b: pe.wait_ge(norm_ready, b + 1), h7)

            def expand_gat(n, q):
                i, r, s = n * QB + q, q % 2, q % RING
                pe.wait_ge(gathered[s], 16 * TQ * (NQ // RING + uses(n, q, RING) + 1))
                pe.wait_ge(loaded[1][s], 16 * (TQ + 2) * (uses(n, q, RING) + 1))
                pe.wait_ge(onehot_t_ready[1], i + 1)
                pe.wait_ge(leaky_ready, i + 1)
                for t in range(TQ):
                    to = bank[r][:, t * P:(t + 1) * P]
                    flip(to, g[:, s * TQ + t, :], stop=False)
                    last = mm(to, win[:, s * TQ + t, :], onehot_t[:, r, t * P:(t + 1) * P], start=False)
                last.then_inc(expanded[1], 1)

            def scores(n, q):
                i, r = n * QB + q, q % 2
                pe.wait_ge(leaky_ready, i + 3)
                pe.wait_ge(alpha_copied, i + 2)
                for t in range(TQ):
                    last = mm(bank[2][:, t * HEADS:(t + 1) * HEADS], hid[:, r, t * P:(t + 1) * P], att_m[:])
                last.then_inc(alpha_done, 1)

            def scores_t(n, q):
                i, r = n * QB + q, q % 2
                pe.wait_ge(alpha_copied, i + 3)
                pe.wait_ge(scan_done, i + 1 + RING - 2)
                flip(bank[(3, 6)[r]][0:TQ * HEADS, 0:P], alpha_s[:, r, :]).then_inc(alpha_t_done, 1)

            def maxima_t(n, q):
                i, r = n * QB + q, q % 2
                pe.wait_ge(scan_done, i + 1 + RING)
                pe.wait_ge(shift_ready, i + 2)
                mm(bank[7][:, 0:TQ * HEADS], seg_max[:, r, :],
                   ident[0:TQ * HEADS, 0:TQ * HEADS]).then_inc(max_t_done, 1)

            sweep(pe, [(scores, 3), (expand_gat, 5), (scores_t, 3), (maxima_t, 2),
                       (sum_partials(1, lambda q, t: msg[:, q % 2, t, :], weighted), 1)])
            for c in range(CH):
                tails_ready(1, c)
                last = flip(bank[c // 4][0:HEADS, (c % 4) * TP:(c % 4 + 1) * TP],
                            tails[:, c, D + HEADS:ROWW])
            last.then_inc(chain_pe, 1)
            pe.wait_ge(chain_dve, 3)
            for c in range(CH):
                last = flip(bank[5][0:TP, c * HEADS:(c + 1) * HEADS], cmax[:, 2, c * TP:(c + 1) * TP])
            last.then_inc(chain_pe, 1)
            pe.wait_ge(chain_dve, 5)
            chain_sums(1)
            project(1, w_ab[:], None, 2 * D, 2, lambda b: pe.wait_ge(norm_ready, NBAT + b + 1), h7)

            def expand_mlp(n, q):
                i, r, s = n * QB + q, q % 2, q % RING
                pe.wait_ge(loaded[2][s], 16 * (TQ + 2) * (uses(n, q, RING) + 1))
                pe.wait_ge(onehot_t_ready[2], i + 1)
                pe.wait_ge(gathered[s], 16 * TQ * (2 * NQ // RING + uses(n, q, RING) + 1))
                pe.wait_ge(hidden_ready, i + 1)
                for t in range(TQ):
                    to = bank[r][:, t * P:(t + 1) * P]
                    flip(to, g[:, s * TQ + t, :], stop=False)
                    mm(to, w1c[:], rel[:, s, t * P:(t + 1) * P], start=False, stop=False)
                    last = mm(to, win[:, s * TQ + t, :], onehot_t[:, r, t * P:(t + 1) * P], start=False)
                last.then_inc(expanded[2], 1)

            def second_layer(n, q):
                i, r = n * QB + q, q % 2
                pe.wait_ge(hidden_ready, i + 3)
                pe.wait_ge(messages_ready, i + 1)
                for t in range(TQ):
                    last = mm(bank[2 + r][:, t * D:(t + 1) * D], hid[:, r, t * P:(t + 1) * P], w2_s[:])
                last.then_inc(hidden_used, 1)

            sweep(pe, [(second_layer, 1), (expand_mlp, 2),
                       (sum_partials(2, lambda q, t: msg[:, q % 2, t, 0:D], messages_ready), 1)])
            chain_sums(2)
            project(2, wn_s[:], b_u_parts, D, 4, lambda b: pe.wait_ge(node_rows, 16 * BT * (2 * NBAT + b + 1)), agg)

            def own_projections(b, q):
                if q == STEP_FLIP:
                    pe.wait_ge(norm_ready, 2 * NBAT + b + 1)
                    pe.wait_ge(xt_copied, 3 * NBAT + b + 1)
                    to_columns(x7, D, 0).then_inc(xt_done, 1)
                if q == STEP_PROJECT:
                    pe.wait_ge(xt_copied, 3 * NBAT + b + 2)
                    for r in range(BT):
                        to = bank[OWN_BANKS[r // 2]][:, (r % 2) * 2 * D:(r % 2 + 1) * 2 * D]
                        mm(to, ht7[:, r, :], w_x[:], stop=False)
                        last = mm(to, ones[0:1, :], b_x[:], start=False)
                    last.then_inc(z_done, 1)

            sweep(pe, [(sum_partials(3, gathered_rhs, None), 0)], 2, own_projections)
            chain_sums(3)
            with pe.Fori(0, NBAT) as b:
                pe.wait_ge(norm_ready, 3 * NBAT + b + 1)
                pe.wait_ge(xt_copied, 4 * NBAT + b + 1)
                to_columns(h7, D, 0).then_inc(xt_done, 1)
                pe.wait_ge(xt_copied, 4 * NBAT + b + 2)
                pe.wait_ge(mix_copied, b + 1)
                for r in range(BT):
                    to = bank[4 + r // 2][:, (r % 2) * 2 * D:(r % 2 + 1) * 2 * D]
                    mm(to, ht7[:, r, :], w_n[:], stop=False)
                    for k in range(2):
                        mm(to[:, k * D:(k + 1) * D], ident[:], own[:, bass.ds(b * BT + r, 1), :].rearrange("p o f -> p (o f)"),
                           start=False, stop=False)
                    last = mm(to, ones_b[:], b_n_parts, start=False)
                last.then_inc(mix_done, 1)

        @block.scalar
        def _(act):
            act.sem_inc(partial_copied, 2)
            act.sem_inc(alpha_copied, 2)
            act.sem_inc(ex_ready, 2)
            act.sem_inc(hidden_ready, 2)
            act.sem_inc(mix_copied, 1)
            for s in (xt_copied, node_out, applied):
                act.sem_inc(s, 1)
            for s in partial_stored + [rows_stored, state_stored, out_stored]:
                act.sem_inc(s, 16)
            act.dma_start(srct[:], src_e).then_inc(src_in, 16)
            act.wait_ge(src_in, 16)
            for s in range(RING):
                nc.scalar.copy(srcq[:, s * TQ:(s + 1) * TQ], srct[:, s * TQ:(s + 1) * TQ]).then_inc(src_idx_ready, 1)
            def put_partials(l):
                def stage(n, q):
                    i, r = n * QB + q, q % 2
                    at, w = NQ * l + i, part_d[l].shape[1]
                    act.wait_ge(partial_done, at + 3)
                    act.wait_ge(partial_stored[r], 16 * ((NQ // 2) * l + uses(n, q, 2) + 1))
                    if l == 1:
                        for h in range(2):
                            last = nc.scalar.copy(part_s[:, r, 2 * h:2 * h + 2, :],
                                                  bank[4 + h][:, 0:2 * w].rearrange("p (t f) -> p t f", f=w))
                    else:
                        last = nc.scalar.copy(part_s[:, r, :, 0:w],
                                              bank[4 + 2 * r][:, :].rearrange("p (t f) -> p t f", f=w))
                    last.then_inc(partial_copied, 1)
                    act.wait_ge(partial_copied, at + 3)
                    act.dma_start(part_d[l][bass.ds(i * QE, QE), :].rearrange("(t s) f -> s t f", s=P),
                                  part_s[:, r, :, 0:w]).then_inc(partial_stored[r], 16)
                return stage

            def refill(used, ahead):
                def stage(n, q):
                    i, s = n * QB + q, q % RING
                    act.wait_ge(used, i + 1 + ahead)
                    nc.scalar.copy(srcq[:, s * TQ:(s + 1) * TQ],
                                   srct[:, bass.ds(i * TQ + RING * TQ, TQ)]).then_inc(src_idx_ready, 1)
                return stage

            def load_columns(l):
                def stage(n, q):
                    i, s = n * QB + q, q % RING
                    act.wait_ge(expanded[l], i + 1)
                    if l == 1:
                        act.wait_ge(scan_done, i + 1)
                    act.dma_start(lrb[:, s, :], bcast(lrank_d[bass.ds(i * TQ, TQ), :].rearrange("t e -> (t e)"), P)
                                  ).then_inc(loaded[l][s], 16)
                    if l == 1:
                        act.dma_start(pen[:, s, :, :].rearrange("p k e -> p (k e)"),
                                      pen_d[bass.ds(i * TQ * HEADS, TQ * HEADS), :]).then_inc(loaded[l][s], 16)
                    else:
                        act.dma_start(rel[0:REL, s, :], rel_t[:, bass.ds(i * QE, QE)]).then_inc(loaded[l][s], 16)
                return stage

            def root(count, k=0):
                act.wait_ge(var_ready, count + 1)
                nc.scalar.activation(std[:, k], var[:, k], ACT.Sqrt).then_inc(std_ready, 1)

            def columns_out(layer, b):
                done = NBAT * layer + b
                act.wait_ge(xt_done, done + 2)
                if layer < 3:
                    act.wait_ge(z_done, done + 1)
                nc.scalar.copy(ht7[:, 0:4, :], bank[0][:, :].rearrange("p (r n) -> p r n", n=P))
                return nc.scalar.copy(ht7[:, 4:BT, :], bank[1][:, 0:3 * P].rearrange("p (r n) -> p r n", n=P))

            def rows_out(layer, b):
                done = NBAT * layer + b
                act.wait_ge(z_done, done + 2)
                act.wait_ge(rows_stored, 16 + 16 * done)
                if not is_batch(done, 0):
                    act.wait_ge(rank_scattered, 16 * BT * done)
                for k in range(4):
                    c = 2 if k < 3 else 1
                    nc.scalar.copy(out7[:, 2 * k:2 * k + c, :],
                                   bank[2 + k][:, 0:c * 2 * D].rearrange("p (r f) -> p r f", f=2 * D))
                nc.scalar.copy(xidx[:], node_xr[:, bass.ds(b * BT, BT)]).then_inc(node_out, 1)

            def project_out(layer, roots):
                def batch_roots(b):
                    for k in range(roots):
                        root((0, 2 * NBAT)[layer] + roots * b + k)

                def step(b):
                    batch_roots(b + 1)
                    rows_out(layer, b)
                    columns_out(layer, b + 1).then_inc(xt_copied, 1)

                batch_roots(0)
                columns_out(layer, 0).then_inc(xt_copied, 1)
                step(0)
                with act.Fori(1, NBAT - 1) as b:
                    step(b)
                rows_out(layer, NBAT - 1)

            sweep(act, [(refill(partial_done, 2), 0), (put_partials(0), 0)])
            act.wait_ge(hist_dve, 3)
            act.wait_ge(zeroed, 16 * 6)
            project_out(0, 2)

            def slopes(n, q):
                i, r = n * QB + q, q % 2
                act.wait_ge(expanded[1], i + 1 + RING)
                act.wait_ge(leaky_ready, i + 1)
                nc.scalar.mul(slope[:, r, :], bank[r][:, :], SLOPE).then_inc(slope_ready, 1)

            def copy_scores(n, q):
                i, r = n * QB + q, q % 2
                act.wait_ge(alpha_done, i + 3)
                act.wait_ge(shift_ready, i + 1)
                nc.scalar.copy(alpha_s[:, r, :], bank[2][:, 0:TQ * HEADS]).then_inc(alpha_copied, 1)

            def exponentials(n, q):
                i, r = n * QB + q, q % 2
                act.wait_ge(shift_ready, i + 3)
                act.wait_ge(weighted, i + 1)
                nc.scalar.activation(ex[:, r, :], shifted[:, r, :], ACT.Exp).then_inc(ex_ready, 1)

            sweep(act, [(slopes, 4), (copy_scores, 3), (put_partials(1), 0), (refill(weighted, 2), 1),
                        (load_columns(1), RING + 1), (exponentials, 2)])
            act.wait_ge(chain_dve, 4)
            nc.scalar.activation(cexp[:, 0], cexp[:, 0], ACT.Exp)
            nc.scalar.activation(cexp[:, 1], cexp[:, 1], ACT.Exp)
            nc.scalar.activation(cexp[:, 2], cexp[:, 2], ACT.Exp).then_inc(chain_act, 1)
            project_out(1, 1)

            def hidden(n, q):
                i, r = n * QB + q, q % 2
                act.wait_ge(expanded[2], i + 1 + RING)
                act.wait_ge(hidden_used, i + 1)
                nc.scalar.activation(hid[:, r, :], bank[r][:, :], ACT.Relu, bias=b1c[:, 0:1]).then_inc(hidden_ready, 1)

            act.wait_ge(rel_cleared, 1)
            sweep(act, [(put_partials(2), 0), (load_columns(2), RING + 1), (hidden, 2),
                        (refill(expanded[2], RING), 2)])
            def apply_norm(of, to, k, count, done, free=None):
                act.wait_ge(scale_ready, count + 1)
                if free is not None:
                    act.wait_ge(free[0], free[1])
                for r in range(BT):
                    last = nc.scalar.activation(to[:, r, :], of[:, r, :], ACT.Identity, bias=nshift[:, k, r:r + 1],
                                                scale=rstd[:, k, r:r + 1])
                last.then_inc(done, 1)

            def inner_norm(b):
                apply_norm(y7, nt7, 0, 0 if is_batch(b, 0) else 2 * b - 1, centred)

            def new_states(b):
                apply_norm(h7, x7, 1, 2 * NBAT - 1 if is_batch(b, NBAT - 1) else 2 * b + 2, applied,
                           (state_stored, 16 + 16 * b))
                act.drain()
                nc.scalar.copy(states(b), x7[:]).then_inc(state_ready, 1)

            columns_out(2, 0).then_inc(xt_copied, 1)
            root(3 * NBAT)
            columns_out(2, 1).then_inc(xt_copied, 1)
            inner_norm(0)
            with act.Fori(1, NBAT - 1) as b:
                root(3 * NBAT + 2 * b - 1)
                columns_out(2, b + 1).then_inc(xt_copied, 1)
                inner_norm(b)
                root(3 * NBAT + 2 * b, 1)
                new_states(b - 1)
            root(3 * NBAT + 2 * (NBAT - 1) - 1)
            inner_norm(NBAT - 1)
            root(3 * NBAT + 2 * (NBAT - 1), 1)
            new_states(NBAT - 2)
            root(3 * NBAT + 2 * NBAT - 1, 1)
            new_states(NBAT - 1)

            def gate(z, k, count):
                act.wait_ge(exp_wanted, count + 1)
                if k == 0:
                    nc.scalar.activation(z[:, 2, :], z[:, 1, :], ACT.Sqrt).then_inc(exp_ready, 1)
                else:
                    nc.scalar.activation(z[:, 2, :], z[:, 1, :], ACT.Exp, scale=(1.0, -1.0)[k - 1]).then_inc(exp_ready, 1)

            def own_columns(b, q):
                if q == STEP_COLUMNS:
                    columns_out(3, b).then_inc(xt_copied, 1)
                if q == STEP_SPLIT:
                    act.wait_ge(z_done, 3 * NBAT + b + 2)
                    act.wait_ge(mix_read, b + 1)
                    for k in range(4):
                        c = 2 if k < 3 else 1
                        z = bank[OWN_BANKS[k]][:, 0:c * 2 * D].rearrange("p (r f) -> p r f", f=2 * D)
                        nc.scalar.copy(own[:, bass.ds(b * BT + 2 * k, c), :], z[:, :, 0:D])
                        nc.scalar.activation(y7[:, 2 * k:2 * k + c, :], z[:, :, D:], ACT.Relu)
                    act.drain()
                    nc.scalar.activation(h7[:], y7[:], ACT.Square).then_inc(split_ready, 1)
                for k, at in enumerate((STEP_ROOT, STEP_EXP, STEP_EXP2)):
                    if q == at:
                        gate(z_id, k, 3 * b + k)

            sweep(act, [(refill(partial_done, 3 * NQ + 2), 0), (put_partials(3), 0)], 2, own_columns)

            def mix_rows(b):
                act.wait_ge(mix_done, b + 1)
                act.wait_ge(mix_read, NBAT + b + 1)
                for k in range(4):
                    c = 2 if k < 3 else 1
                    last = nc.scalar.activation(mix[:, 2 * k:2 * k + c, :],
                                                bank[4 + k][:, 0:c * 2 * D].rearrange("p (r f) -> p r f", f=2 * D), ACT.Relu)
                last.then_inc(mix_copied, 1)

            def squares(b):
                act.drain()
                nc.scalar.activation(mix_sq[:], mix, ACT.Square).then_inc(square_ready, 1)

            def gates(b):
                for k in range(3):
                    gate(z_mix, k, 3 * NBAT + 3 * b + k)

            def results(b):
                apply_norm(y7, x7, 0, 2 * NBAT + b, out_ready, (out_stored, 16 + 16 * b))

            def mix_step(b):
                mix_rows(b)
                if not is_batch(b, NBAT - 1):
                    columns_out(4, b + 1).then_inc(xt_copied, 1)
                first = is_batch(b, 0)
                if not first:
                    root(5 * NBAT + b - 1)
                squares(b)
                gates(b)
                if not first:
                    results(b - 1)

            columns_out(4, 0).then_inc(xt_copied, 1)
            mix_step(0)
            with act.Fori(1, NBAT - 1) as b:
                mix_step(b)
            mix_step(NBAT - 1)
            root(5 * NBAT + NBAT - 1)
            results(NBAT - 1)

        @block.vector
        def _(dve):
            v = nc.vector
            dve.sem_inc(leaky_ready, 2)
            dve.sem_inc(scan_done, RING)
            for s in (shift_ready, weighted, messages_ready):
                dve.sem_inc(s, 2)
            for s in (update_read, mix_read):
                dve.sem_inc(s, 1)
            v.memset(zeros[:], 0.0).then_inc(zeros_made, 1)
            dve.wait_ge(consts_made, 1)
            v.tensor_copy(iota_row[:], iota_i[:])
            v.tensor_copy(iota_col[:], iota_ci[:])

            dve.wait_ge(tables_in, 16 * 6)
            v.tensor_copy(dtf, dti)
            v.tensor_copy(dpf, dpi)
            v.tensor_copy(dnf, dni)
            v.tensor_copy(lrow, lrow_i)
            v.tensor_copy(tsm[:, 8, :], tail0_i[:, 0, :])
            v.tensor_copy(tsm[:, 9, :], tail0_i[:, 1, :])
            v.tensor_scalar(hilo_i[:, 0, :], dst_ei, 7, None, ALU.arith_shift_right)
            v.tensor_scalar(hilo_i[:, 1, :], dst_ei, P - 1, None, ALU.bitwise_and)
            dve.drain()
            v.tensor_copy(rec[:, :, HI], hilo_i[:, 0, :])
            v.tensor_copy(rec[:, :, LO], hilo_i[:, 1, :])
            v.tensor_tensor(chg, dtf, dpf, ALU.not_equal)
            v.tensor_tensor(lastf, dtf, dnf, ALU.not_equal)
            dve.drain()
            v.tensor_reduce(tsm[:, 0, :], chg, AX_X, ALU.add)
            v.tensor_copy(loc, chg)
            v.tensor_copy(tsm[:, 1, :], chg[:, :, 0])
            dve.drain()
            dve.sem_inc(prep_dve, 1)
            v.memset(loc[:, :, 0], 0.0)
            v.memset(chg[:, :, 0], 1.0)
            v.tensor_scalar(tsm[:, 2, :], lastf[:, :, P - 1], -1.0, 1.0, ALU.mult, ALU.add)
            dve.drain()
            for c in range(CH):
                v.tensor_tensor_scan(lrank[:, c, :], loc[:, c, :], zeros[0:TP, 0:P], 0.0, ALU.add, ALU.max)
            dve.wait_ge(prep_pe, 1)
            v.tensor_tensor_scan(tsm[:, 3, :], bank[4][0:TP, CH:2 * CH], zeros[0:TP, 0:CH], 0.0, ALU.add, ALU.max)
            dve.drain()
            v.tensor_tensor(tsm[:, 4, :], tsm[:, 3, :], bank[4][0:TP, CH:2 * CH], ALU.subtract)
            dve.drain()
            v.tensor_tensor(tsm[:, 4, :], tsm[:, 4, :], bank[4][0:TP, 0:CH], ALU.add)
            dve.drain()
            v.scalar_tensor_tensor(out=tsm[:, 4, :], in0=tsm[:, 4, :], scalar=-1.0, in1=tsm[:, 1, :], op0=ALU.add, op1=ALU.add)
            dve.drain()
            v.tensor_copy(rank0_s[:], tsm[:, 4, :])
            v.tensor_tensor(slotf, lrank, tsm[:, 4, :].unsqueeze(2).broadcast_to([TP, CH, P]), ALU.add)
            dve.drain()
            v.tensor_copy(sloti, slotf)
            dve.drain()
            v.tensor_scalar(sloti, sloti, P - 1, None, ALU.bitwise_and)
            dve.drain()
            v.tensor_copy(slotf, sloti)
            v.tensor_copy(lrank_b, lrank)
            dve.drain()
            dve.sem_inc(prep_dve, 1)
            v.tensor_scalar(loc, loc, -BIG, None, ALU.mult)
            v.tensor_scalar(lastf, lastf, -BIG, None, ALU.mult)
            v.tensor_tensor(tsm[:, 5, :], tsm[:, 8, :], slotf[:, :, P - 1], ALU.add)
            dve.drain()
            dve.sem_inc(rows_ready, 1)
            v.tensor_copy(tail_i[:], tsm[:, 5, :])
            v.scalar_tensor_tensor(out=tsm[:, 6, :], in0=tsm[:, 5, :], scalar=float(P), in1=tsm[:, 9, :],
                                   op0=ALU.add, op1=ALU.subtract)
            dve.drain()
            v.tensor_tensor(tsm[:, 6, :], tsm[:, 6, :], tsm[:, 2, :], ALU.mult)
            dve.drain()
            v.tensor_tensor(head_i[:], tsm[:, 6, :], tsm[:, 9, :], ALU.add)
            dve.wait_ge(prep_pe, 2)
            for field, k in ((SLOT, 0), (FIRST, 2)):
                v.tensor_copy(rec[:, 0:4 * TP, field], bank[k][:, 0:4 * TP])
                v.tensor_copy(rec[:, 4 * TP:NT, field], bank[k + 1][:, 0:3 * TP])
            v.tensor_copy(rec[:, :, WEIGHT], wcol)
            dve.drain()
            dve.sem_inc(prep_dve, 1)

            def one_hots(l):
                def stage(n, q):
                    i, r = n * QB + q, q % 2
                    v.tensor_copy(crec[:, r], rec[:, bass.ds(i * TQ, TQ), :])
                    dve.drain()
                    dve.wait_ge(partial_done, NQ * l + i + 1)
                    for t in range(TQ):
                        if l == 0:
                            last = v.tensor_scalar(onehot[:, r, t, :], iota_row[:], crec[:, r, t, SLOT:SLOT + 1],
                                                   crec[:, r, t, WEIGHT:WEIGHT + 1], ALU.is_equal, ALU.mult)
                        else:
                            last = v.tensor_scalar(onehot[:, r, t, :], iota_row[:], crec[:, r, t, SLOT:SLOT + 1],
                                                   None, ALU.is_equal)
                    last.then_inc(onehot_ready, 1)
                return stage

            def hist_one_hots(n, q):
                i, r = n * QB + q, q % 2
                dve.wait_ge(hist_done, i + 1)
                for t in range(TQ):
                    v.tensor_scalar(hi1[:, r, t, :], iota_row[:, 0:NB], crec[:, r, t, HI:HI + 1], None, ALU.is_equal)
                    last = v.tensor_scalar(lo1[:, r, t, :], iota_row[:], crec[:, r, t, LO:LO + 1], None, ALU.is_equal)
                last.then_inc(hist_ready, 1)

            def transposed_one_hots(l, per_quad):
                def stage(n, q):
                    i, r, s = n * QB + q, q % 2, q % RING
                    dve.wait_ge(loaded[l][s], 16 * per_quad * (uses(n, q, RING) + 1))
                    dve.wait_ge(expanded[l], i + 1 + RING - 2)
                    v.tensor_scalar(onehot_t[:, r, :], lrb[:, s, :], iota_col[:, 0:1], None,
                                    ALU.is_equal).then_inc(onehot_t_ready[l], 1)
                return stage

            def chain_out_of_psum(l):
                for k in range(2):
                    dve.wait_ge(chain_pe, {0: 1, 2: 6, 3: 8}[l] + k)
                    c0, c1 = 4 * k, min(CH, 4 * k + 4)
                    v.tensor_copy(heads[:, c0:c1, 0:D],
                                  bank[k][0:TP, 0:(c1 - c0) * D].rearrange("p (c f) -> p c f", f=D)).then_inc(chain_dve, 1)

            def norm_stats(of, k=0):
                for r in range(BT):
                    v.bn_stats(bst[:, r, :], of[:, r, :])
                dve.drain()
                for r in range(BT):
                    v.bn_aggr(mv[:, k, r, :], bst[:, r, :])
                dve.drain()
                v.tensor_scalar(var[:, k], mv[:, k, :, 1], EPS, None, ALU.add).then_inc(var_ready, 1)

            def norm_scale(count, k=0):
                r1 = rstd[:, k]
                dve.wait_ge(std_ready, count + 1)
                v.reciprocal(r1, std[:, k])
                dve.drain()
                v.scalar_tensor_tensor(out=nwt[:], in0=r1, scalar=-0.5, in1=r1, op0=ALU.mult, op1=ALU.mult)
                dve.drain()
                v.tensor_tensor(nwt[:], nwt[:], var[:, k], ALU.mult)
                dve.drain()
                v.scalar_tensor_tensor(out=r1, in0=nwt[:], scalar=1.5, in1=r1, op0=ALU.add, op1=ALU.mult)
                dve.drain()

            def norm_shift(count, k=0):
                norm_scale(count, k)
                v.scalar_tensor_tensor(out=nshift[:, k], in0=mv[:, k, :, 0], scalar=-1.0, in1=rstd[:, k],
                                       op0=ALU.mult, op1=ALU.mult)
                dve.drain()
                dve.sem_inc(scale_ready, 1)

            def layer_norm(to, of, count):
                norm_stats(of)
                norm_scale(count)
                for r in range(BT):
                    v.tensor_scalar(to[:, r, :], of[:, r, :], mv[:, 0, r, 0:1], rstd[:, 0, r:r + 1], ALU.subtract, ALU.mult)
                dve.drain()

            def next_indices(b):
                v.tensor_copy(nidx[:], node_row[:, bass.ds(b * BT + BT, BT)]).then_inc(node_idx_ready, 1)

            def bc7(v2):
                return v2.unsqueeze(1).broadcast_to([P, BT, D])

            sweep(dve, [(one_hots(0), 0), (hist_one_hots, 0)])
            dve.wait_ge(weights_in, 16 * N_WEIGHTS)
            v.tensor_copy(lnb3[:], lnb[:, 0:1].broadcast_to([P, 3])).then_inc(prep_dve, 1)
            for c2 in range(CH):
                for c in range(c2 + 1):
                    v.tensor_scalar(chain_m[:, c2 * (c2 + 1) // 2 + c, :], lrow[:, c2 * TP:(c2 + 1) * TP],
                                    dtf[:, c, P - 1:P], None, ALU.is_equal)
            dve.drain()
            for c in range(CH):
                k = c * (c + 1) // 2 + c
                v.tensor_tensor(chain_m[:, k, :], chain_m[:, k, :], trieq[0:TP, 0:TP], ALU.mult)
            v.memset(penc[:], -BIG)
            dve.drain()
            v.tensor_tensor(penc[:, 0, 1:], lrow[0:HEADS, 1:], lrow[0:HEADS, 0:NT - 1], ALU.not_equal)
            v.tensor_tensor(penc[:, 1, 0:NT - 1], lrow[0:HEADS, 1:], lrow[0:HEADS, 0:NT - 1], ALU.not_equal)
            dve.drain()
            v.tensor_scalar(penc[:, 0, 1:], penc[:, 0, 1:], -BIG, None, ALU.mult)
            v.tensor_scalar(penc[:, 1, 0:NT - 1], penc[:, 1, 0:NT - 1], -BIG, None, ALU.mult)
            dve.wait_ge(hist_done, NQ + 2)
            v.tensor_copy(hist[:, 0, :], bank[3][0:NB, 0:P])
            dve.drain()
            v.tensor_scalar(hist[:, 1, :], hist[:, 0, :], 0.0, None, ALU.is_gt)
            dve.drain()
            v.tensor_reduce(htot[:, 0:1], hist[:, 0, :], AX_X, ALU.add)
            v.tensor_reduce(htot[:, 1:2], hist[:, 1, :], AX_X, ALU.add)
            v.tensor_tensor_scan(hist[:, 2, :], hist[:, 0, :], zeros[0:NB, 0:P], 0.0, ALU.add, ALU.max)
            v.tensor_tensor_scan(hist[:, 3, :], hist[:, 1, :], zeros[0:NB, 0:P], 0.0, ALU.add, ALU.max)
            v.tensor_copy(hist[:, 4, :], xr0_i[:])
            dve.drain()
            dve.sem_inc(hist_dve, 1)
            dve.wait_ge(hist_pe, 1)
            v.tensor_copy(htot[:], bank[2][0:NB, 0:2])
            dve.drain()
            v.tensor_scalar(hist[:, 2, :], hist[:, 2, :], htot[:, 0:1], -1.0, ALU.add, ALU.add)
            v.scalar_tensor_tensor(out=hist[:, 3, :], in0=hist[:, 3, :], scalar=htot[:, 1:2], in1=hist[:, 1, :],
                                   op0=ALU.add, op1=ALU.subtract)
            dve.drain()
            v.tensor_copy(histi[:, 0, :], hist[:, 2, :])
            v.tensor_copy(histi[:, 1, :], hist[:, 3, :])
            dve.drain()
            v.tensor_scalar(histi[:, 0, :], histi[:, 0, :], 7, 7, ALU.arith_shift_right, ALU.logical_shift_left)
            v.tensor_scalar(histi[:, 1, :], histi[:, 1, :], P - 1, None, ALU.bitwise_and)
            dve.drain()
            v.tensor_copy(hist[:, 5, :], histi[:, 0, :])
            v.tensor_copy(hist[:, 2, :], histi[:, 1, :])
            v.tensor_tensor(hist[:, 6, :], hist[:, 3, :], hist[:, 4, :], ALU.subtract)
            v.tensor_scalar(hist[:, 7, :], hist[:, 0, :], 1.0, None, ALU.max)
            dve.drain()
            v.scalar_tensor_tensor(out=hist[:, 5, :], in0=hist[:, 5, :], scalar=float(-ZROW), in1=hist[:, 2, :],
                                   op0=ALU.add, op1=ALU.add)
            v.tensor_tensor(hist[:, 6, :], hist[:, 6, :], hist[:, 1, :], ALU.mult)
            v.reciprocal(hist[:, 7, :], hist[:, 7, :])
            dve.drain()
            v.tensor_tensor(hist[:, 5, :], hist[:, 5, :], hist[:, 1, :], ALU.mult)
            v.tensor_tensor(hist[:, 6, :], hist[:, 6, :], hist[:, 4, :], ALU.add)
            dve.drain()
            v.tensor_scalar(hist[:, 5, :], hist[:, 5, :], float(ZROW), None, ALU.add)
            dve.drain()
            dve.sem_inc(hist_dve, 1)
            dve.wait_ge(hist_pe, 2)
            v.tensor_copy(node_row[:, 0:NB], bank[2][:, P:P + NB])
            v.tensor_copy(node_row[:, NB:NB + BT], bank[2][:, P:P + BT])
            v.tensor_copy(node_xr[:], bank[2][:, P + NB:P + 2 * NB])
            v.tensor_copy(rdeg[:], bank[2][:, P + 2 * NB:P + 3 * NB])
            dve.drain()
            dve.sem_inc(hist_dve, 1)
            v.tensor_copy(nidx[:], node_row[:, 0:BT]).then_inc(node_idx_ready, 1)
            dve.wait_ge(prep_pe, 3)
            v.tensor_tensor(b_lr, b_lr, bank[5][0:3, 0:2 * D], ALU.add)
            v.tensor_scalar(w_lr[:], w_lr[:], lng[:, 0:1], None, ALU.mult)
            v.tensor_scalar(att_m[:], hmask[:], attc[:, 0:1], None, ALU.mult)
            v.tensor_scalar(w_n[:, D:], w_n[:, D:], -1.0, None, ALU.mult)
            v.tensor_scalar(b_n[:, D:], b_n[:, 0:D], -1.0, None, ALU.mult)
            v.memset(w1c[REL:P, :], 0.0)
            dve.drain()
            high, rest, middle = (nview(buf, 3)[:, 0:5 * D] for buf in (x7, h7, y7))
            for part, of in ((high, biases[:]), (middle, rest)):
                v.tensor_copy(bias_parts[0:3], of)
                dve.drain()
                v.tensor_copy(part, bias_parts[0:3])
                dve.drain()
                v.tensor_tensor(rest, of, part, ALU.subtract)
                dve.drain()
            v.tensor_scalar(high, high, ident[0:3, 0:1], None, ALU.mult)
            dve.drain()
            v.scalar_tensor_tensor(out=middle, in0=middle, scalar=ident[0:3, 1:2], in1=high, op0=ALU.mult, op1=ALU.add)
            dve.drain()
            v.scalar_tensor_tensor(out=rest, in0=rest, scalar=ident[0:3, 2:3], in1=middle, op0=ALU.mult, op1=ALU.add)
            dve.drain()
            v.tensor_copy(bias_parts[0:3], rest)
            dve.drain()
            dve.wait_ge(x_in, 16)
            chain_out_of_psum(0)
            with dve.Fori(0, NBAT) as b:
                dve.wait_ge(node_rows, 16 * BT * (b + 1))
                v.tensor_tensor(y7[:], agg[:, :, 0:D], states(b), ALU.add)
                dve.drain()
                next_indices(b)
                layer_norm(x7, y7, 2 * b)
                v.tensor_copy(states(b), x7[:])
                dve.wait_ge(xt_done, b + 1)
                layer_norm(h7, x7, 2 * b + 1)
                dve.sem_inc(norm_ready, 1)

            def leaky(n, q):
                i, r = n * QB + q, q % 2
                dve.wait_ge(slope_ready, i + 1)
                dve.wait_ge(alpha_done, i + 1)
                v.tensor_tensor(hid[:, r, :], bank[r][:, :], slope[:, r, :], ALU.max).then_inc(leaky_ready, 1)

            def run_maxima(n, q):
                i, r, s = n * QB + q, q % 2, q % RING
                dve.wait_ge(alpha_t_done, i + 1)
                dve.wait_ge(max_t_done, i + 1)
                v.tensor_tensor_scan(fwd[:], pen[:, s, 0, :], bank[(3, 6)[r]][0:TQ * HEADS, 0:P],
                                     -BIG, ALU.add, ALU.max)
                dve.drain()
                v.tensor_tensor_scan(seg_max[:, r, ::-1], pen[:, s, 1, ::-1], fwd[:, ::-1],
                                     -BIG, ALU.add, ALU.max).then_inc(scan_done, 1)

            def shift(n, q):
                i, r = n * QB + q, q % 2
                top = bank[7][:, 0:TQ * HEADS]
                v.tensor_copy(cfirst[:, r, :], rec[:, bass.ds(i * TQ, TQ), FIRST])
                dve.drain()
                dve.wait_ge(max_t_done, i + 3)
                dve.wait_ge(ex_ready, i + 1)
                dve.wait_ge(partial_done, NQ + i + 1)
                v.tensor_tensor(msg[:, r, :, D + HEADS:], top.rearrange("p (t h) -> p t h", h=HEADS),
                                cfirst[:, r, :].unsqueeze(2).broadcast_to([P, TQ, HEADS]), ALU.mult)
                v.tensor_tensor(shifted[:, r, :], alpha_s[:, r, :], top, ALU.subtract).then_inc(shift_ready, 1)

            def weigh(n, q):
                i, r, s = n * QB + q, q % 2, q % RING
                dve.wait_ge(ex_ready, i + 3)
                exr = ex[:, r, :].rearrange("p (t h) -> p t h", h=HEADS)
                v.tensor_copy(msg[:, r, :, D:D + HEADS], exr)
                v.tensor_tensor(msg[:, r, :, 0:D].rearrange("p t (h c) -> p t h c", c=HC),
                                g[:, s * TQ:(s + 1) * TQ, :].rearrange("p t (h c) -> p t h c", c=HC),
                                exr.unsqueeze(3).broadcast_to([P, TQ, HEADS, HC]), ALU.mult).then_inc(weighted, 1)

            sweep(dve, [(weigh, 1), (run_maxima, 2), (leaky, 4), (one_hots(1), 2), (shift, 2),
                        (transposed_one_hots(1, TQ + 2), 6)])

            tail_m, head_m = tails[:, :, D + HEADS:], heads[:, :, D + HEADS:]
            dve.wait_ge(chain_pe, 3)
            dve.wait_ge(heads_in, 16 * CH)
            v.tensor_copy(cmax[:, 0, 0:4 * TP], bank[0][0:HEADS, 0:4 * TP])
            v.tensor_copy(cmax[:, 0, 4 * TP:NT], bank[1][0:HEADS, 0:3 * TP])
            dve.drain()
            v.tensor_tensor_scan(cmax[:, 1, :], penc[:, 0, :], cmax[:, 0, :], -BIG, ALU.add, ALU.max)
            dve.drain()
            v.tensor_tensor_scan(cmax[:, 2, ::-1], penc[:, 1, ::-1], cmax[:, 1, ::-1], -BIG, ALU.add, ALU.max)
            dve.drain()
            dve.sem_inc(chain_dve, 1)
            dve.wait_ge(chain_pe, 4)
            top = bank[5][0:TP, 0:CH * HEADS].rearrange("p (c h) -> p c h", h=HEADS)
            v.tensor_tensor(cexp[:, 0], tail_m, top, ALU.subtract)
            v.tensor_tensor(cexp[:, 3], head_m, top, ALU.max)
            dve.drain()
            v.tensor_tensor(cexp[:, 1], top, cexp[:, 3], ALU.subtract)
            v.tensor_tensor(cexp[:, 2], head_m, cexp[:, 3], ALU.subtract)
            dve.drain()
            dve.sem_inc(chain_dve, 1)
            dve.wait_ge(chain_act, 1)

            def per_head(buf, c0, c1):
                return buf[:, c0:c1, 0:D].rearrange("p c (h k) -> p c h k", k=HC)

            def over_channels(k, c0, c1):
                return cexp[:, k, c0:c1, :].unsqueeze(3).broadcast_to([TP, c1 - c0, HEADS, HC])

            for buf, k in ((tails, 0), (heads, 2)):
                v.tensor_tensor(per_head(buf, 0, CH), per_head(buf, 0, CH), over_channels(k, 0, CH), ALU.mult)
                v.tensor_tensor(buf[:, :, D:D + HEADS], buf[:, :, D:D + HEADS], cexp[:, k], ALU.mult)
            v.tensor_copy(head_m, cexp[:, 3])
            dve.drain()
            dve.sem_inc(chain_dve, 1)
            dve.wait_ge(chain_pe, 5)
            for k in range(3):
                c0, c1 = 3 * k, min(CH, 3 * k + 3)
                z = bank[k][0:TP, 0:(c1 - c0) * (D + HEADS)].rearrange("p (c f) -> p c f", f=D + HEADS)
                v.tensor_tensor(per_head(tails, c0, c1), per_head(z, 0, c1 - c0), over_channels(1, c0, c1), ALU.mult)
                v.tensor_tensor(tails[:, c0:c1, D:D + HEADS], z[:, :, D:], cexp[:, 1, c0:c1, :], ALU.mult)
            dve.drain()
            v.tensor_tensor(heads[:, :, 0:D + HEADS], heads[:, :, 0:D + HEADS], tails[:, :, 0:D + HEADS], ALU.add)
            dve.drain()
            dve.sem_inc(chain_dve, 1)
            with dve.Fori(0, NBAT) as b:
                dve.wait_ge(node_rows, 16 * BT * (NBAT + b + 1))
                v.tensor_scalar(rden[:], agg[:, :, D:D + HEADS], 1e-16, None, ALU.add)
                dve.drain()
                v.reciprocal(rden[:], rden[:])
                dve.drain()
                v.tensor_tensor(y7[:].rearrange("p b (h c) -> p b h c", c=HC),
                                agg[:, :, 0:D].rearrange("p b (h c) -> p b h c", c=HC),
                                rden[:].unsqueeze(3).broadcast_to([P, BT, HEADS, HC]), ALU.mult)
                dve.drain()
                next_indices(b)
                v.tensor_tensor(y7[:], y7[:], bc7(biasg_b[:]), ALU.add)
                dve.drain()
                v.tensor_scalar(y7[:], y7[:], 0.0, None, ALU.max)
                dve.drain()
                v.scalar_tensor_tensor(out=y7[:], in0=states(b), scalar=2.0, in1=y7[:], op0=ALU.mult, op1=ALU.add)
                dve.drain()
                dve.wait_ge(xt_done, NBAT + b + 1)
                layer_norm(h7, y7, 2 * NBAT + b)
                v.tensor_copy(states(b), h7[:])
                dve.drain()
                dve.sem_inc(norm_ready, 1)

            v.memset(rel[REL:P, :, :], 0.0).then_inc(rel_cleared, 1)

            def messages(n, q):
                i, r = n * QB + q, q % 2
                dve.wait_ge(hidden_used, i + 3)
                dve.wait_ge(partial_done, 2 * NQ + i + 1)
                to = msg[:, r, :, 0:D]
                v.tensor_tensor(to, bank[2 + r][:, :].rearrange("p (t f) -> p t f", f=D),
                                b2_b[:].unsqueeze(1).broadcast_to([P, TQ, D]), ALU.add)
                dve.drain()
                v.tensor_scalar(to, to, 0.0, None, ALU.max).then_inc(messages_ready, 1)

            sweep(dve, [(messages, 1), (transposed_one_hots(2, TQ + 2), 3), (one_hots(2), 2)])
            chain_out_of_psum(2)

            def updated(b):
                dve.wait_ge(z_done, 2 * NBAT + b + 2)
                if not is_batch(b, 0):
                    dve.wait_ge(centred, b)
                for k in range(2):
                    c = (4, 3)[k]
                    last = v.scalar_tensor_tensor(
                        out=y7[:, 4 * k:4 * k + c, :], in0=bank[2 + k][:, 0:c * D].rearrange("p (r f) -> p r f", f=D),
                        scalar=0.0, in1=xa[:, bass.ds(b * BT + 4 * k, c), :], op0=ALU.max, op1=ALU.add)
                last.then_inc(update_read, 1)
                dve.drain()
                norm_stats(y7)

            def summed(b):
                dve.wait_ge(xt_done, 2 * NBAT + b + 2)
                next_indices(b)

            def scaled(b):
                dve.wait_ge(centred, b + 1)
                dve.wait_ge(applied, b + 1)
                v.tensor_tensor(h7[:], nt7[:], bc7(gamma_b[:]), ALU.mult)
                dve.drain()

            def residual(b):
                v.tensor_tensor(h7[:], h7[:], bc7(beta_b[:]), ALU.add)
                dve.drain()
                v.tensor_tensor(h7[:], h7[:], states(b), ALU.add)
                dve.drain()
                norm_stats(h7, 1)

            summed(0)
            updated(0)
            norm_shift(3 * NBAT)
            summed(1)

            def two_norms(b):
                updated(b)
                scaled(b - 1)
                norm_shift(3 * NBAT + 2 * b - 1)
                if not is_batch(b, NBAT - 1):
                    summed(b + 1)
                residual(b - 1)
                norm_shift(3 * NBAT + 2 * b, 1)

            with dve.Fori(1, NBAT - 1) as b:
                two_norms(b)
            two_norms(NBAT - 1)
            scaled(NBAT - 1)
            residual(NBAT - 1)
            norm_shift(3 * NBAT + 2 * NBAT - 1, 1)

            def squared_norm(z):
                v.tensor_scalar(z[:, 1, :], z[:, 1, :], 1e-34, None, ALU.max)
                dve.drain()
                dve.sem_inc(exp_wanted, 1)

            def score(z, k, count):
                ab = ab_b[:, 2:3] if k == 1 else ab_b[:, 0:2]
                dve.wait_ge(exp_ready, count + 1)
                v.reciprocal(z[:, 3, :], z[:, 2, :])
                dve.drain()
                v.tensor_tensor(z[:, 3, :], z[:, 3, :], z[:, 1, :], ALU.mult)
                dve.drain()
                v.tensor_tensor(z[:, 3, :], z[:, 3, :], z[:, 2, :], ALU.add)
                dve.drain()
                v.tensor_scalar(z[:, 3, :], z[:, 3, :], 0.5, 1e-16, ALU.mult, ALU.add)
                dve.drain()
                v.reciprocal(z[:, 3, :], z[:, 3, :])
                dve.drain()
                v.tensor_tensor(z[:, 0, :], z[:, 0, :], z[:, 3, :], ALU.mult)
                dve.drain()
                v.tensor_tensor(z[:, 0, :].rearrange("p (b k) -> p b k", k=k), z[:, 0, :].rearrange("p (b k) -> p b k", k=k),
                                ab.unsqueeze(1).broadcast_to([P, BT, k]), ALU.add)
                dve.drain()
                v.tensor_scalar(z[:, 1, :], z[:, 0, :], 0.0, None, ALU.min)
                v.tensor_scalar(z[:, 4, :], z[:, 0, :], 0.0, -5.0, ALU.max, ALU.add)
                dve.drain()
                dve.sem_inc(exp_wanted, 1)

            def elu(z, count):
                dve.wait_ge(exp_ready, count + 2)
                v.scalar_tensor_tensor(out=z[:, 1, :], in0=z[:, 2, :], scalar=5.0, in1=z[:, 4, :],
                                       op0=ALU.mult, op1=ALU.add)
                dve.drain()
                dve.sem_inc(exp_wanted, 1)

            def sigmoid(z, count):
                dve.wait_ge(exp_ready, count + 3)
                v.tensor_scalar(z[:, 3, :], z[:, 2, :], 1.0, None, ALU.add)
                dve.drain()
                v.reciprocal(z[:, 3, :], z[:, 3, :])
                dve.drain()
                v.tensor_scalar(z[:, 3, :], z[:, 3, :], 3.0, None, ALU.mult)
                dve.drain()

            def own_gate(b, q):
                if q == STEP_STATES:
                    dve.wait_ge(xt_done, 3 * NBAT + b + 1)
                    v.tensor_copy(x7[:], states(b)).then_inc(norm_ready, 1)
                if q == STEP_DOTS:
                    dve.wait_ge(split_ready, b + 1)
                    v.tensor_tensor(nt7[:], y7[:], bc7(a_b[:, 2 * D:]), ALU.mult)
                    v.tensor_reduce(z_id[:, 1, :], h7[:], AX_X, ALU.add)
                    dve.drain()
                    v.tensor_reduce(z_id[:, 0, :], nt7[:], AX_X, ALU.add)
                    squared_norm(z_id)
                if q == STEP_SCORE:
                    score(z_id, 1, 3 * b)
                if q == STEP_ELU:
                    elu(z_id, 3 * b)
                if q == STEP_MIX:
                    sigmoid(z_id, 3 * b)
                    v.tensor_tensor(y7[:], y7[:], z_id[:, 3, :].unsqueeze(2).broadcast_to([P, BT, D]), ALU.mult)
                    dve.drain()
                    v.tensor_tensor(states(b), states(b), y7[:], ALU.add)
                    dve.drain()
                    dve.sem_inc(mix_read, 1)

            dve.wait_ge(state_stored, 16 + 16 * NBAT)
            sweep(dve, [(one_hots(3), 0)], 2, own_gate)
            chain_out_of_psum(3)

            def neighbours(b):
                dve.wait_ge(node_rows, 16 * BT * (3 * NBAT + b + 1))
                dve.wait_ge(xt_done, 4 * NBAT + b + 1)
                v.tensor_tensor(h7[:], agg[:, :, 0:D],
                                rdeg[:, bass.ds(b * BT, BT)].unsqueeze(2).broadcast_to([P, BT, D]), ALU.mult)
                dve.drain()
                dve.sem_inc(norm_ready, 1)
                next_indices(b)

            parts = "p b (k f) -> p (b k) f"

            def dots(b):
                dve.wait_ge(mix_copied, b + 2)
                v.tensor_tensor(mix_a, mix, a_b[:, 0:2 * D].unsqueeze(1).broadcast_to([P, BT, 2 * D]), ALU.mult)
                dve.drain()
                v.tensor_reduce(z_mix[:, 0, :], mix_a.rearrange(parts, k=2), AX_X, ALU.add)

            def gates(b):
                count = 3 * NBAT + 3 * b
                dve.wait_ge(square_ready, b + 1)
                v.tensor_reduce(z_mix[:, 1, :], mix_sq[:].rearrange(parts, k=2), AX_X, ALU.add)
                dve.drain()
                squared_norm(z_mix)
                score(z_mix, 2, count)
                elu(z_mix, count)
                sigmoid(z_mix, count)
                v.tensor_tensor(mix_a.rearrange(parts, k=2), mix.rearrange(parts, k=2),
                                z_mix[:, 3, :].unsqueeze(2).broadcast_to([P, BT * 2, D]), ALU.mult)
                dve.drain()
                dve.sem_inc(mix_read, 1)
                v.tensor_tensor(nt7[:], mix_a[:, :, 0:D], mix_a[:, :, D:], ALU.add)
                dve.drain()
                if not is_batch(b, 0):
                    dve.wait_ge(out_ready, b)
                v.tensor_tensor(y7[:], nt7[:], states(b), ALU.add)
                dve.drain()
                norm_stats(y7)

            neighbours(0)
            neighbours(1)
            dots(0)
            gates(0)
            with dve.Fori(1, NBAT - 1) as b:
                neighbours(b + 1)
                dots(b)
                norm_shift(5 * NBAT + b - 1)
                gates(b)
            dots(NBAT - 1)
            norm_shift(5 * NBAT + NBAT - 2)
            gates(NBAT - 1)
            norm_shift(5 * NBAT + NBAT - 1)


def kernel(**inputs):
    import numpy as np
    import concourse.bacc as bacc
    from concourse.bass_utils import run_bass_kernel_spmd

    def flat(name, count, fill):
        a = np.asarray(inputs[name])
        return np.concatenate([a, np.full((count - a.shape[0],) + a.shape[1:], fill, a.dtype)])

    dst = flat("dst", EPAD, NODES)
    edge = np.asarray([NODES + 1], dst.dtype)
    src = flat("src", EPAD, 0).reshape(NT, P).T
    arrays = {
        "x": flat("x", NPAD, 0),
        "src_e": np.concatenate([src, src[:, 0:RING * TQ]], axis=1),
        "dst_t": dst.reshape(NT, P),
        "prev_t": np.concatenate([edge, dst[:-1]]).reshape(NT, P),
        "next_t": np.concatenate([dst[1:], edge]).reshape(NT, P),
        "dst_e": dst.reshape(NT, P).T,
        "last_row": dst.reshape(NT, P)[:, P - 1],
        "weight_e": flat("edge_weight", EPAD, 0).reshape(NT, P).T,
        "rel_t": flat("edge_attr_64", EPAD, 0).T,
    }
    for name in ("L1_gnn_ln_g", "L1_gnn_ln_b", "L1_gnn_W_l", "L1_gnn_b_l", "L1_gnn_W_r", "L1_gnn_b_r", "L1_gnn_att",
                 "L1_gnn_bias", "L2_gnn_W1", "L2_gnn_b1", "L2_gnn_W2", "L2_gnn_b2", "L2_gnn_Wn", "L2_gnn_bn",
                 "L2_gnn_gamma", "L2_gnn_beta", "L3_gnn_w_self", "L3_gnn_b_self", "L3_gnn_w_neigh", "L3_gnn_b_neigh",
                 "L3_gnn_w_id", "L3_gnn_b_id", "L3_gnn_a_low", "L3_gnn_ab_low", "L3_gnn_a_high", "L3_gnn_ab_high",
                 "L3_gnn_a_id", "L3_gnn_ab_id"):
        arrays[name[7:]] = np.asarray(inputs[name])
    arrays = {n: np.ascontiguousarray(a) for n, a in arrays.items()}

    nc = bacc.Bacc("TRN2", target_bir_lowering=False, num_devices=1)
    args = {n: nc.dram_tensor(f"in_{n}", a.shape, mybir.dt.from_np(a.dtype), kind="ExternalInput").ap()
            for n, a in arrays.items()}
    res = nc.dram_tensor("out_x", (NPAD, D), F32, kind="ExternalOutput").ap()
    gnn_program(nc, out=res, **args)
    r = run_bass_kernel_spmd(nc, [{f"in_{n}": a for n, a in arrays.items()}], core_ids=[0])
    return r.results[0]["out_x"][:NODES]
```
